# Optimizing a Trainium2 kernel written in Bass

```python
import numpy as np
import jax
import jax.numpy as jnp

def _softmax(x, axis=-1):
    return jax.nn.softmax(x, axis=axis)

def _gelu(x):
    return jax.nn.gelu(x, approximate=True)

def _silu(x):
    return jax.nn.silu(x)

def _sigmoid(x):
    return jax.nn.sigmoid(x)

def _layernorm(x, axis=-1, eps=1e-05):
    m = jnp.mean(x, axis=axis, keepdims=True)
    v = jnp.var(x, axis=axis, keepdims=True)
    return (x - m) / jnp.sqrt(v + eps)

def _scatter_add(tgt, idx, src, axis=0):
    return tgt.at[idx].add(src)

def _segment_sum(src, seg, n):
    return jax.ops.segment_sum(src, seg, n)
kernel_name = 'mk_seq_preln_d2_jaxref_r8_2072d0'

def setup_inputs(seed: int=0):
    np.random.seed(seed)
    _w = jnp.asarray

    def _L0_attn_setup():
        import jax, jax.numpy as jnp
        import numpy as np
        HEADS = 16
        DIMS = [64, 64, 64, 64]
        EPS = 0.0001
        P_POW = 2

        def _cdist(Q, K):
            q2 = jnp.sum(Q * Q, axis=-1)
            k2 = jnp.sum(K * K, axis=-1)
            qk = jnp.einsum('hbtd,hbsd->hbts', Q, K)
            d2 = q2[..., :, None] + k2[..., None, :] - 2.0 * qk
            return jnp.sqrt(jnp.maximum(d2, 0.0))
        key = jax.random.key(seed)
        ks = jax.random.split(key, 4)
        b, t, d_in = (2, 256, 128)
        d_proj = HEADS * sum(DIMS)
        X = jax.random.normal(ks[0], (b, t, d_in), dtype=jnp.float32)
        W_in = jax.random.normal(ks[1], (d_in, d_proj), dtype=jnp.float32) * d_in ** (-0.5)
        b_in = jnp.zeros((d_proj,), dtype=jnp.float32)
        W_out = jax.random.normal(ks[2], (HEADS * DIMS[2], d_in), dtype=jnp.float32) * (HEADS * DIMS[2]) ** (-0.5)
        b_out = jnp.zeros((d_in,), dtype=jnp.float32)
        return {'X': X, 'W_in': W_in, 'b_in': b_in, 'W_out': W_out, 'b_out': b_out}
    _L0_attn_in = _L0_attn_setup()

    def _L0_ffn_setup():
        import jax, jax.numpy as jnp
        import numpy as np
        BLOCK = 16
        _GRID = jnp.array([0.0, 0.5, 1.0, 1.5, 2.0, 3.0, 4.0, 6.0], dtype=jnp.float32)
        _MID = jnp.array([0.25, 0.75, 1.25, 1.75, 2.5, 3.5, 5.0], dtype=jnp.float32)

        def fp4_quant_dequant(x):
            shape = x.shape
            xb = x.reshape(shape[:-1] + (shape[-1] // BLOCK, BLOCK))
            scale = jnp.max(jnp.abs(xb), axis=-1, keepdims=True) / 6.0
            scale = jnp.maximum(scale, jnp.float32(1e-12))
            xn = xb / scale
            idx = jnp.searchsorted(_MID, jnp.abs(xn))
            q = _GRID[idx] * jnp.sign(xn) * scale
            return q.reshape(shape)

        def fp4_linear(x, w):
            xq = fp4_quant_dequant(x)
            wq = fp4_quant_dequant(w)
            return jnp.einsum('bsk,nk->bsn', xq, wq)
        key = jax.random.key(seed)
        k1, k2, k3, k4 = jax.random.split(key, 4)
        H, I = (128, 352)
        x = jax.random.normal(k1, (4, 512, H), dtype=jnp.float32)
        w_gate = jax.random.normal(k2, (I, H), dtype=jnp.float32) * 0.02
        w_up = jax.random.normal(k3, (I, H), dtype=jnp.float32) * 0.02
        w_down = jax.random.normal(k4, (H, I), dtype=jnp.float32) * 0.02
        return {'x': x, 'w_gate': w_gate, 'w_up': w_up, 'w_down': w_down}
    _L0_ffn_in = _L0_ffn_setup()

    def _L1_attn_setup():
        import jax, jax.numpy as jnp
        import numpy as np
        import math
        B, S, E = (2, 256, 128)
        H, DK, DV = (16, 64, 64)

        def _rope(q, k):
            D = q.shape[-1]
            theta = 10000.0 ** (jnp.arange(0, D, 2, dtype=jnp.float32) / D)
            pos = jnp.arange(q.shape[-2], dtype=jnp.float32)
            freqs = pos[:, None] * (1.0 / theta)[None, :]
            emb = jnp.concatenate([freqs, freqs], axis=-1)
            cos = jnp.cos(emb)[None, None]
            sin = jnp.sin(emb)[None, None]

            def rotate(x):
                x1 = x[..., ::2]
                x2 = x[..., 1::2]
                return jnp.stack([-x2, x1], axis=-1).reshape(x.shape)
            return (q * cos + rotate(q) * sin, k * cos + rotate(k) * sin)
        key = jax.random.key(seed)
        ks = jax.random.split(key, 9)
        sE = 1.0 / math.sqrt(E)
        sV = 1.0 / math.sqrt(H * DV)
        return {'x': jax.random.normal(ks[0], (B, S, E), dtype=jnp.float32), 'wq': jax.random.uniform(ks[1], (H * DK, E), jnp.float32, -sE, sE), 'bq': jax.random.uniform(ks[2], (H * DK,), jnp.float32, -sE, sE), 'wk': jax.random.uniform(ks[3], (H * DK, E), jnp.float32, -sE, sE), 'bk': jax.random.uniform(ks[4], (H * DK,), jnp.float32, -sE, sE), 'wv': jax.random.uniform(ks[5], (H * DV, E), jnp.float32, -sE, sE), 'bv': jax.random.uniform(ks[6], (H * DV,), jnp.float32, -sE, sE), 'wo': jax.random.uniform(ks[7], (E, H * DV), jnp.float32, -sV, sV), 'bo': jax.random.uniform(ks[8], (E,), jnp.float32, -sV, sV)}
    _L1_attn_in = _L1_attn_setup()

    def _L1_ffn_setup():
        import jax, jax.numpy as jnp
        import numpy as np
        B, N, D = (4, 256, 128)
        SPARSITY = 0.01
        key = jax.random.key(seed)
        k1, k2, k3 = jax.random.split(key, 3)
        x = jax.random.normal(k1, (B, N, D), dtype=jnp.float32)
        spatial = jax.random.normal(k2, (D, D), dtype=jnp.float32) * 0.02
        freq = jnp.fft.fft(spatial, axis=-1)
        k = int(D * SPARSITY)
        mag = jnp.abs(freq)
        kth = jax.lax.top_k(mag, k)[0][:, -1:]
        w_sparse = jnp.where(mag >= kth, freq, 0.0 + 0j)
        bias = jax.random.normal(k3, (D,), dtype=jnp.float32) * 0.01
        return {'x': x, 'w_freq_real': jnp.real(w_sparse).astype(jnp.float32), 'w_freq_imag': jnp.imag(w_sparse).astype(jnp.float32), 'bias': bias}
    _L1_ffn_in = _L1_ffn_setup()
    _d = {'L0_attn_X': _L0_attn_in['X'], 'L0_attn_W_in': _L0_attn_in['W_in'], 'L0_attn_b_in': _L0_attn_in['b_in'], 'L0_attn_W_out': _L0_attn_in['W_out'], 'L0_attn_b_out': _L0_attn_in['b_out'], 'L0_ffn_w_gate': _L0_ffn_in['w_gate'], 'L0_ffn_w_up': _L0_ffn_in['w_up'], 'L0_ffn_w_down': _L0_ffn_in['w_down'], 'L1_attn_wq': _L1_attn_in['wq'], 'L1_attn_bq': _L1_attn_in['bq'], 'L1_attn_wk': _L1_attn_in['wk'], 'L1_attn_bk': _L1_attn_in['bk'], 'L1_attn_wv': _L1_attn_in['wv'], 'L1_attn_bv': _L1_attn_in['bv'], 'L1_attn_wo': _L1_attn_in['wo'], 'L1_attn_bo': _L1_attn_in['bo'], 'L1_ffn_w_freq_real': _L1_ffn_in['w_freq_real'], 'L1_ffn_w_freq_imag': _L1_ffn_in['w_freq_imag'], 'L1_ffn_bias': _L1_ffn_in['bias']}
    _x0 = _d['L0_attn_X']
    _d['L0_attn_X'] = jax.random.normal(jax.random.fold_in(jax.random.key(seed), 1), (1, 2048, 128), dtype=_x0.dtype)
    del _x0
    return _d

def reference(L0_attn_X, L0_attn_W_in, L0_attn_b_in, L0_attn_W_out, L0_attn_b_out, L0_ffn_w_gate, L0_ffn_w_up, L0_ffn_w_down, L1_attn_wq, L1_attn_bq, L1_attn_wk, L1_attn_bk, L1_attn_wv, L1_attn_bv, L1_attn_wo, L1_attn_bo, L1_ffn_w_freq_real, L1_ffn_w_freq_imag, L1_ffn_bias):

    def _L0_attn_ref(X, W_in, b_in, W_out, b_out):
        import jax, jax.numpy as jnp
        import numpy as np
        HEADS = 16
        DIMS = [64, 64, 64, 64]
        EPS = 0.0001
        P_POW = 2

        def _cdist(Q, K):
            q2 = jnp.sum(Q * Q, axis=-1)
            k2 = jnp.sum(K * K, axis=-1)
            qk = jnp.einsum('hbtd,hbsd->hbts', Q, K)
            d2 = q2[..., :, None] + k2[..., None, :] - 2.0 * qk
            return jnp.sqrt(jnp.maximum(d2, 0.0))
        b, t, _ = X.shape
        P = X @ W_in + b_in
        P = P.reshape(b, t, HEADS, sum(DIMS))
        P = jnp.transpose(P, (2, 0, 1, 3))
        splits = np.cumsum(DIMS)[:-1]
        Q, K, V, G = jnp.split(P, splits, axis=-1)
        W = jnp.power(EPS + _cdist(Q, K), -P_POW)
        W = W / (EPS + jnp.sum(W, axis=-1, keepdims=True))
        A = jnp.einsum('hbts,hbse->hbte', W, V)
        H = G * A
        H = jnp.transpose(H, (1, 2, 0, 3)).reshape(b, t, HEADS * DIMS[2])
        return H @ W_out + b_out

    def _L0_ffn_ref(x, w_gate, w_up, w_down):
        import jax, jax.numpy as jnp
        import numpy as np
        BLOCK = 16
        _GRID = jnp.array([0.0, 0.5, 1.0, 1.5, 2.0, 3.0, 4.0, 6.0], dtype=jnp.float32)
        _MID = jnp.array([0.25, 0.75, 1.25, 1.75, 2.5, 3.5, 5.0], dtype=jnp.float32)

        def fp4_quant_dequant(x):
            shape = x.shape
            xb = x.reshape(shape[:-1] + (shape[-1] // BLOCK, BLOCK))
            scale = jnp.max(jnp.abs(xb), axis=-1, keepdims=True) / 6.0
            scale = jnp.maximum(scale, jnp.float32(1e-12))
            xn = xb / scale
            idx = jnp.searchsorted(_MID, jnp.abs(xn))
            q = _GRID[idx] * jnp.sign(xn) * scale
            return q.reshape(shape)

        def fp4_linear(x, w):
            xq = fp4_quant_dequant(x)
            wq = fp4_quant_dequant(w)
            return jnp.einsum('bsk,nk->bsn', xq, wq)
        gate = fp4_linear(x, w_gate)
        y = fp4_linear(x, w_up)
        h = jax.nn.silu(gate) * y
        return fp4_linear(h, w_down)

    def _L1_attn_ref(x, wq, bq, wk, bk, wv, bv, wo, bo):
        import jax, jax.numpy as jnp
        import numpy as np
        import math
        B, S, E = (2, 256, 128)
        H, DK, DV = (16, 64, 64)

        def _rope(q, k):
            D = q.shape[-1]
            theta = 10000.0 ** (jnp.arange(0, D, 2, dtype=jnp.float32) / D)
            pos = jnp.arange(q.shape[-2], dtype=jnp.float32)
            freqs = pos[:, None] * (1.0 / theta)[None, :]
            emb = jnp.concatenate([freqs, freqs], axis=-1)
            cos = jnp.cos(emb)[None, None]
            sin = jnp.sin(emb)[None, None]

            def rotate(x):
                x1 = x[..., ::2]
                x2 = x[..., 1::2]
                return jnp.stack([-x2, x1], axis=-1).reshape(x.shape)
            return (q * cos + rotate(q) * sin, k * cos + rotate(k) * sin)
        Bx, Sx, Ex = x.shape
        q = (x @ wq.T + bq).reshape(Bx, Sx, H, DK).transpose(0, 2, 1, 3)
        k = (x @ wk.T + bk).reshape(Bx, Sx, H, DK).transpose(0, 2, 1, 3)
        v = (x @ wv.T + bv).reshape(Bx, Sx, H, DV).transpose(0, 2, 1, 3)
        q, k = _rope(q, k)
        scores = jnp.einsum('bhqd,bhkd->bhqk', q, k)
        causal = jnp.triu(jnp.ones((Sx, Sx), dtype=bool), k=1)
        scores = jnp.where(causal[None, None], -jnp.inf, scores)
        attn = jax.nn.softmax(scores / math.sqrt(DK), axis=-1)
        out = jnp.einsum('bhqk,bhkd->bhqd', attn, v)
        out = out.transpose(0, 2, 1, 3).reshape(Bx, Sx, H * DV)
        return out @ wo.T + bo

    def _L1_ffn_ref(x, w_freq_real, w_freq_imag, bias):
        import jax, jax.numpy as jnp
        import numpy as np
        B, N, D = (4, 256, 128)
        SPARSITY = 0.01
        w = jax.lax.complex(w_freq_real, w_freq_imag)
        x_freq = jnp.fft.fft(x, axis=-1)
        y_freq = jnp.einsum('bnd,do->bno', x_freq, w)
        y = jnp.real(jnp.fft.ifft(y_freq, axis=-1))
        return y + bias
    x = L0_attn_X
    x = x + _L0_attn_ref(_layernorm(x, axis=-1), L0_attn_W_in, L0_attn_b_in, L0_attn_W_out, L0_attn_b_out)
    x = x + _L0_ffn_ref(_layernorm(x, axis=-1), L0_ffn_w_gate, L0_ffn_w_up, L0_ffn_w_down)
    x = x + _L1_attn_ref(_layernorm(x, axis=-1), L1_attn_wq, L1_attn_bq, L1_attn_wk, L1_attn_bk, L1_attn_wv, L1_attn_bv, L1_attn_wo, L1_attn_bo)
    x = x + _L1_ffn_ref(_layernorm(x, axis=-1), L1_ffn_w_freq_real, L1_ffn_w_freq_imag, L1_ffn_bias)
    return x

_drawn_inputs = setup_inputs


def setup_inputs(seed=0):
    import zlib

    import numpy as np

    out = dict(_drawn_inputs(seed))
    spreads = {'L0_attn_b_in': (0.0, 0.1), 'L0_attn_b_out': (0.0, 0.1)}
    factors = {'L0_ffn_w_gate': 5.569,
     'L0_ffn_w_up': 5.309,
     'L0_ffn_w_down': 5.334,
     'L1_attn_wq': 6.141,
     'L1_attn_bq': 8.0,
     'L1_attn_wk': 6.017,
     'L1_attn_bk': 8.0,
     'L1_attn_bo': 2.958,
     'L1_ffn_bias': 6.269,
     'L1_attn_bv': 4.241}
    for name, (base, spread) in spreads.items():
        noise = np.random.default_rng([zlib.crc32(name.encode()), seed]).standard_normal(out[name].shape)
        drawn = base * np.exp(spread * noise) if base else spread * noise
        out[name] = jnp.asarray(drawn.astype(out[name].dtype))
    for name, factor in factors.items():
        out[name] = (out[name] * factor).astype(out[name].dtype)
    return out
```

```python
import numpy as np

import concourse.bass as bass
from concourse import mybir
from contextlib import ExitStack

F32 = mybir.dt.float32
F32R = mybir.dt.float32r
BF16 = mybir.dt.bfloat16
ALU = mybir.AluOpType
ACT = mybir.ActivationFunctionType
AX = mybir.AxisListType

P = 128
T = 2048
E = 128
HEADS = 16
DH = 64
TILES = T // P
QB = 512
BLOCKS = T // QB
LN_EPS = 1e-5
UNITS = TILES // 2
STEPS = 2 * BLOCKS
PW = 7 * DH + 3 + DH
OFF_K, OFF_G, OFF_V, OFF_B, OFF_BV = 2 * DH, 4 * DH, 6 * DH, 7 * DH, 7 * DH + 3
AUX = 4
AUXP = 32
INNER = 352
CHUNKS = 4
CHUNK = INNER // CHUNKS
FP4_BLOCK = 16
FP4_MIDDLES = (0.25, 0.75, 1.25, 1.75, 2.5, 3.5, 5.0)
CW = 2 * P + DH + 2 + DH
CB, CV = 2 * P + DH, 2 * P + DH + 2
MASK_0 = QB - P
MASK_Q = MASK_0 + QB
MASKS = MASK_Q + P
TABLE = 69
LOG_EXP_SET = "natural_log_exp_and_others"


def layer_norm(nc, ctx, x, xnT, identity, name):
    xn = ctx.enter_context(nc.sbuf_tensor(f"{name}_xn", [P, TILES, E], F32))
    stats = ctx.enter_context(nc.sbuf_tensor(f"{name}_stats", [P, TILES, 6], F32))
    moments = ctx.enter_context(nc.sbuf_tensor(f"{name}_moments", [P, TILES, 2], F32))
    std = ctx.enter_context(nc.sbuf_tensor(f"{name}_std", [P, TILES], F32))
    rstd = ctx.enter_context(nc.sbuf_tensor(f"{name}_rstd", [P, TILES], F32))
    eps = ctx.enter_context(nc.sbuf_tensor(f"{name}_eps", [P, 1], F32))
    if xnT is not None:
        flipped = ctx.enter_context(nc.psum_tensor(f"{name}_flipped", [P, 2, QB], F32))
    have_stats = ctx.enter_context(nc.semaphore(f"{name}_have_stats"))
    have_moments = ctx.enter_context(nc.semaphore(f"{name}_have_moments"))
    have_std = ctx.enter_context(nc.semaphore(f"{name}_have_std"))
    have_rstd = ctx.enter_context(nc.semaphore(f"{name}_have_rstd"))
    have_rows = ctx.enter_context(nc.semaphore(f"{name}_have_rows"))
    have_flipped = ctx.enter_context(nc.semaphore(f"{name}_have_flipped"))
    copied = ctx.enter_context(nc.semaphore(f"{name}_copied"))
    with nc.Block() as block:
        @block.vector
        def _(dve):
            dve.memset(eps[:, :], LN_EPS)
            for t in range(TILES):
                dve.bn_stats(stats[:, t, :], x[:, t, :]).then_inc(have_stats, 1)
            for t in range(TILES):
                dve.wait_ge(have_stats, t + 1)
                dve.bn_aggr(moments[:, t, :], stats[:, t, :]).then_inc(have_moments, 1)
            dve.wait_ge(have_std, 1)
            dve.reciprocal(rstd[:, :], std[:, :]).then_inc(have_rstd, 1)
            dve.wait_ge(have_rstd, 1)
            for t in range(TILES):
                dve.tensor_scalar(xn[:, t, :], x[:, t, :], moments[:, t, 0:1], rstd[:, t:t + 1],
                                  ALU.subtract, ALU.mult).then_inc(have_rows, 1)

        @block.scalar
        def _(act):
            act.wait_ge(have_moments, TILES)
            act.activation(std[:, :], moments[:, :, 1], ACT.Sqrt, bias=eps[:, 0:1]).then_inc(have_std, 1)
            if xnT is not None:
                for b in range(BLOCKS):
                    act.wait_ge(have_flipped, 4 * b + 4)
                    act.activation(xnT[:, b * QB:(b + 1) * QB], flipped[:, b % 2, :], ACT.Copy).then_inc(copied, 1)

        if xnT is not None:
            @block.tensor
            def _(pe):
                for t in range(TILES):
                    b = t // 4
                    if t % 4 == 0 and b >= 2:
                        pe.wait_ge(copied, b - 1)
                    pe.wait_ge(have_rows, t + 1)
                    pe.transpose(flipped[:, b % 2, (t % 4) * P:(t % 4 + 1) * P], xn[:, t, :],
                                 identity[:, :]).then_inc(have_flipped, 1)
    return xn


def distance_attention(nc, ctx, x, xnT, heads_in, heads_out, table, identity):
    def sb(name, shape, dt=F32):
        return ctx.enter_context(nc.sbuf_tensor(f"da_{name}", shape, dt))

    def ps(name, shape):
        return ctx.enter_context(nc.psum_tensor(f"da_{name}", shape, F32))

    def sem(name):
        return ctx.enter_context(nc.semaphore(f"da_{name}"))

    EPS = 1e-4
    head_w = sb("head_w", [P, 2, PW])
    head_o = sb("head_o", [P, 2, E])
    k_split = sb("k_split", [P, 2, T], F32R)
    k_high = sb("k_high", [P, 2, T], F32R)
    q_high = sb("q_high", [P, 2, QB], F32R)
    q_low = sb("q_low", [P, 2, QB], F32R)
    values = sb("values", [P, 2, TILES, DH])
    gates = sb("gates", [P, STEPS, QB])
    weights = sb("weights", [P, 2 * UNITS, 2 * QB])
    sums = sb("sums", [P, 2, 2 * QB])
    gated = sb("gated", [P, 2, QB])
    k_full = sb("k_full", [P, QB])
    q_full = sb("q_full", [P, QB])
    k_square = sb("k_square", [P, QB])
    q_square = sb("q_square", [P, QB])
    aux_high = sb("aux_high", [P, 2, QB], F32R)
    den = sb("den", [P, 2, 4])
    rden = sb("rden", [P, 2, 4])
    ones = sb("ones", [P, 1])
    primer = sb("primer", [P, 6])
    eps = sb("eps", [P, 1])

    scores = ps("scores", [P, 2, 2 * QB])
    mixed = ps("mixed", [P, 2, QB])
    side = ps("side", [P, 2, QB])

    loaded_w = [sem("loaded_w0"), sem("loaded_w1")]
    loaded_o = [sem("loaded_o0"), sem("loaded_o1")]
    primed = sem("primed")
    scored = sem("scored")
    clipped = sem("clipped")
    rooted = sem("rooted")
    logged = sem("logged")
    weighed = sem("weighed")
    mixing = sem("mixing")
    summed = sem("summed")
    folded = sem("folded")
    side_full = [sem("side_full0"), sem("side_full1")]
    side_free = [sem("side_free0"), sem("side_free1")]
    k_copied = sem("k_copied")
    q_copied = sem("q_copied")
    k_squared = sem("k_squared")
    q_squared = sem("q_squared")
    k_rounded = sem("k_rounded")
    q_rounded = sem("q_rounded")
    aux_rounded = sem("aux_rounded")
    rden_done = sem("rden_done")
    gate_done = sem("gate_done")
    block = ctx.enter_context(nc.Block())

    sel_k, sel_q = table[:, 0:AUXP], table[:, AUXP:2 * AUXP]
    rows = slice(DH, DH + AUXP)
    add_k, keep_k = table[rows, 64:65], table[rows, 65:66]
    add_q, keep_q = table[rows, 66:67], table[rows, 67:68]
    TURNS = HEADS // 2
    PRE = [2 * BLOCKS, BLOCKS + 1]

    def value_of(b):
        parity, j = divmod(b, BLOCKS)
        return (parity, j + BLOCKS - 2) if j < 2 else (1 - parity, j - 2)


    @block.sync
    def _(sp):
        def load_w(parity, head):
            sp.dma_start(head_w[:, parity, :], heads_in[head]).then_inc(loaded_w[parity], 16)

        def load_o(parity, head):
            sp.dma_start(head_o[:, parity, :], heads_out[head]).then_inc(loaded_o[parity], 16)

        load_w(0, 0)
        load_w(1, 1)
        load_o(0, 0)
        load_o(1, 1)
        with sp.Fori(0, TURNS) as turn:
            first_out = sp.snap(turn * (4 * STEPS) + PRE[1] + 4 * 2 + 4)
            first_in = sp.snap(turn * (4 * STEPS) + PRE[0] + 4 * 2 + 2)
            second_out = sp.snap(turn * (4 * STEPS) + PRE[1] + 4 * 6 + 4)
            second_in = sp.snap(turn * (4 * STEPS) + PRE[0] + 4 * 6 + 2)
            sp.wait_ge(side_free[0], first_in)
            load_w(0, turn * 2 + 2)
            sp.wait_ge(side_free[1], first_out)
            load_o(1, turn * 2 + 1)
            sp.wait_ge(side_free[1], second_out)
            load_o(0, turn * 2 + 2)
            sp.wait_ge(side_free[0], second_in)
            load_w(1, turn * 2 + 3)
        for s in loaded_w:
            sp.wait_ge(s, 16 * (TURNS + 1))
        for s in loaded_o:
            sp.wait_ge(s, 16 * (TURNS + 1))

    @block.tensor
    def _(pe):
        def piece(bank, n):
            pe.wait_ge(side_free[bank], n)
            return side[:, bank, :]

        def project(bank, n, parity, col, j):
            pe.matmul(piece(bank, n), head_w[:, parity, col:col + P], xnT[:, j * QB:(j + 1) * QB],
                      start=True, stop=True).then_inc(side_full[bank], 1)

        def project_v(bank, n, parity, j):
            out = piece(bank, n)
            for i in range(4):
                t = 4 * j + i
                last = pe.matmul(out[:, i * DH:(i + 1) * DH], xnT[:, t * P:(t + 1) * P],
                                 head_w[:, parity, OFF_V:OFF_V + DH], start=True, stop=True)
            last.then_inc(side_full[bank], 1)

        def norms(bank, n, sel, square):
            out = piece(bank, n)
            pe.matmul(out[rows, :], sel, square[:, :], start=True, stop=True).then_inc(side_full[bank], 1)

        def total(bank, n, slot):
            out = piece(bank, n)
            for i in range(4):
                last = pe.matmul(out[:, i:i + 1], sums[:, slot, i * P:(i + 1) * P], ones[:, :],
                                 start=True, stop=True)
            last.then_inc(side_full[bank], 1)

        def project_out(bank, n, slot, parity):
            out = piece(bank, n)
            for i in range(4):
                last = pe.matmul(out[:, i * P:(i + 1) * P], gated[:, slot, i * P:(i + 1) * P],
                                 head_o[:, parity, :], start=True, stop=True)
            last.then_inc(side_full[bank], 1)

        def distances(parity, slot, k):
            for half in range(2):
                c = 2 * k + half
                out = scores[:, k % 2, half * QB:(half + 1) * QB]
                pe.matmul(out, k_split[:, parity, c * P:(c + 1) * P], q_high[:, slot, :],
                          start=True, stop=False)
                last = pe.matmul(out, k_high[0:DH + AUXP, parity, c * P:(c + 1) * P],
                                 q_low[0:DH + AUXP, slot, :], start=False, stop=True)
            last.then_inc(scored, 1)

        def mix(parity, slot, k):
            for half in range(2):
                last = pe.matmul(mixed[half * DH:(half + 1) * DH, slot, :],
                                 values[:, parity, 2 * k + half, :],
                                 weights[:, slot * UNITS + k, half * QB:(half + 1) * QB],
                                 start=k == 0, stop=k == UNITS - 1)
            last.then_inc(mixing, 1)

        pe.wait_ge(primed, 1)
        pe.wait_ge(loaded_w[0], 16)
        pe.wait_ge(loaded_o[1], 16)
        for j in range(BLOCKS):
            if j == 0:
                pe.matmul(side[:, 0, :], head_w[:, 0, OFF_K:OFF_K + P], xnT[:, 0:QB],
                          start=True, stop=True).then_inc(side_full[0], 1)
            else:
                project(0, j + min(j, 2), 0, OFF_K, j)
            if j < BLOCKS - 2:
                project_v(0, 2 * j + 1, 0, j)
            pe.wait_ge(k_squared, j + 1)
            if j == 0:
                pe.matmul(side[rows, 1, :], sel_k, k_square[:, :], start=True, stop=True).then_inc(side_full[1], 1)
            else:
                norms(1, j, sel_k, k_square)
        project(1, BLOCKS, 0, 0, 0)
        project(0, BLOCKS + 2, 0, OFF_G, 0)
        pe.wait_ge(q_squared, 1)
        norms(0, BLOCKS + 3, sel_q, q_square)

        with pe.Fori(0, TURNS) as turn:
            for b in range(STEPS):
                parity, j = divmod(b, BLOCKS)
                step = turn * STEPS + b
                n0, n1 = turn * (4 * STEPS) + PRE[0] + 4 * b, turn * (4 * STEPS) + PRE[1] + 4 * b
                q_parity, qj = (b + 1) // BLOCKS % 2, (b + 1) % BLOCKS
                for k in range(UNITS):
                    if k == 0:
                        pe.wait_ge(side_free[0], n0)
                    pe.wait_ge(clipped, turn * (STEPS * UNITS) + b * UNITS + k + 1)
                    distances(parity, b % 2, k)
                    if k == 0:
                        pe.wait_ge(gate_done, step + 1)
                        if b % BLOCKS == 2:
                            pe.wait_ge(side_free[1], n1 - 2)
                    if k % 2 == 0:
                        pe.wait_ge(weighed, turn * (STEPS * BLOCKS) + b * BLOCKS + k // 2 + 1)
                    mix((b - 2) // BLOCKS % 2, b % 2, k)
                    if k == 0:
                        if j == 0:
                            pe.wait_ge(loaded_w[1 - parity], turn * 16 + 16 + 16 * parity)
                        project(0, n0, 1 - parity, OFF_K, j)
                    if k == 1:
                        project(1, n1, q_parity, 0, qj)
                    if k == 2:
                        project(0, n0 + 1, q_parity, OFF_G, qj)
                    if k == 3:
                        project_v(1, n1 + 1, *value_of(b))
                    if k == 4:
                        pe.wait_ge(k_squared, step + BLOCKS + 1)
                        norms(0, n0 + 2, sel_k, k_square)
                    if k == 5:
                        pe.wait_ge(q_squared, step + 2)
                        norms(1, n1 + 2, sel_q, q_square)
                    if k == 6:
                        pe.wait_ge(folded, step + 1)
                        total(0, n0 + 3, (b - 3) % 2)
                    if k == 7:
                        pe.wait_ge(gate_done, step + 2)
                        if b % BLOCKS == 3:
                            pe.wait_ge(loaded_o[parity], turn * 16 + 16 + 16 * parity)
                        project_out(1, n1 + 3, (b - 3) % 2, (b - 3) // BLOCKS % 2)

        steps = TURNS * STEPS
        for b in range(3):
            step, n0, n1 = steps + b, PRE[0] + 4 * steps + b, PRE[1] + 4 * steps + b
            if b < 2:
                pe.wait_ge(gate_done, step + 1)
                for k in range(UNITS):
                    if k % 2 == 0:
                        pe.wait_ge(weighed, step * BLOCKS + k // 2 + 1)
                    mix(1, b, k)
            pe.wait_ge(folded, step + 1)
            total(0, n0, (b - 3) % 2)
            pe.wait_ge(gate_done, step + 2)
            project_out(1, n1, (b - 3) % 2, 1)

    @block.scalar
    def _(act):
        act.wait_ge(primed, 1)
        with act.Fori(0, TURNS) as turn:
            for b in range(STEPS):
                pairs = turn * (STEPS * BLOCKS) + b * BLOCKS
                s0 = (b % 2) * UNITS
                for i in range(UNITS // 2):
                    act.wait_ge(clipped, turn * (STEPS * UNITS) + b * UNITS + 2 * i + 4)
                    w = weights[:, s0 + 2 * i:s0 + 2 * i + 2, :]
                    act.activation(w, w, ACT.Sqrt).then_inc(rooted, 1)
                act.preload_act_table_set(LOG_EXP_SET)
                for i in range(UNITS // 2):
                    act.wait_ge(rooted, pairs + i + 1)
                    w = weights[:, s0 + 2 * i:s0 + 2 * i + 2, :]
                    act.activation(w, w, ACT.Ln, bias=eps[:, 0:1]).then_inc(logged, 1)
                for i in range(UNITS // 2):
                    act.wait_ge(logged, pairs + i + 1)
                    w = weights[:, s0 + 2 * i:s0 + 2 * i + 2, :]
                    act.activation(w, w, ACT.Exp, scale=-2.0).then_inc(weighed, 1)

    @block.gpsimd
    def _(pool):
        def sum_block(slot, n, pairs, units):
            total = sums[:, slot, :]
            for k in range(1, UNITS):
                if k == 1 or k % 2 == 0:
                    pool.wait_ge(weighed, pairs + k // 2 + 1)
                if k == 1:
                    pool.wait_ge(rden_done, n)
                    pool.tensor_tensor(total, weights[:, slot * UNITS, :], weights[:, slot * UNITS + 1, :],
                                       ALU.add).then_inc(summed, 2)
                else:
                    pool.wait_ge(summed, units + k)
                    pool.tensor_tensor(total, total, weights[:, slot * UNITS + k, :],
                                       ALU.add).then_inc(summed, 1)
            pool.wait_ge(summed, units + UNITS)
            pool.tensor_tensor(total[:, 0:QB], total[:, 0:QB], total[:, QB:2 * QB], ALU.add).then_inc(folded, 1)

        pool.memset(weights[:, :, :], 0.0)
        pool.memset(values[:, 1, :, :], 0.0)
        pool.memset(gates[:, STEPS - 3:STEPS, :], 0.0)
        pool.memset(sums[:, :, :], 0.0).then_inc(folded, 2)
        pool.memset(ones[:, :], 1.0)
        pool.memset(eps[:, :], EPS)
        pool.memset(primer[:, 4:5], 0.0).then_inc(primed, 1)
        pool.memset(primer[:, 0:1], 0.0).then_inc(weighed, UNITS)
        pool.memset(primer[:, 1:2], 0.0).then_inc(summed, UNITS)
        with pool.Fori(0, TURNS) as turn:
            for b in range(STEPS):
                step = turn * STEPS + b
                sum_block((b - 1) % 2, step + 2, turn * (STEPS * BLOCKS) + (b + 1) * BLOCKS,
                          turn * (STEPS * UNITS) + b * UNITS + UNITS)
        steps = TURNS * STEPS
        sum_block(1, steps + 2, (steps + 1) * BLOCKS, steps * UNITS + UNITS)

    @block.vector
    def _(dve):
        def projected(full, bank, n, bias, copied):
            dve.wait_ge(side_full[bank], n + 1)
            dve.tensor_scalar(full[:, :], side[:, bank, :], bias, None, ALU.add).then_inc(copied, 1)

        def keys(bank, n, parity, j, count):
            cols = slice(j * QB, (j + 1) * QB)
            projected(k_full, bank, n, head_w[:, parity, OFF_B + 1:OFF_B + 2], k_copied)
            dve.wait_ge(k_copied, count + 1)
            dve.tensor_copy(k_split[:, parity, cols], k_full[:, :]).then_inc(k_rounded, 1)
            dve.tensor_tensor(k_square[:, :], k_full[:, :], k_full[:, :], ALU.mult).then_inc(k_squared, 1)
            dve.tensor_copy(k_high[0:DH, parity, cols], k_full[0:DH, :]).then_inc(side_free[bank], 1)
            dve.wait_ge(k_rounded, count + 1)
            dve.tensor_tensor(k_split[DH:P, parity, cols], k_full[DH:P, :],
                              k_split[DH:P, parity, cols].bitcast(F32), ALU.subtract)

        def queries(bank, n, parity, slot, count):
            projected(q_full, bank, n, head_w[:, parity, OFF_B:OFF_B + 1], q_copied)
            dve.wait_ge(q_copied, count + 1)
            dve.tensor_copy(q_high[:, slot, :], q_full[:, :]).then_inc(q_rounded, 1)
            dve.tensor_tensor(q_square[:, :], q_full[:, :], q_full[:, :], ALU.mult).then_inc(q_squared, 1)
            dve.wait_ge(q_rounded, count + 1)
            dve.tensor_tensor(q_low[0:DH, slot, :], q_full[0:DH, :], q_high[0:DH, slot, :].bitcast(F32),
                              ALU.subtract).then_inc(side_free[bank], 1)

        def rank_four(bank, n, out, add, keep, count, high):
            dve.wait_ge(side_full[bank], n + 1)
            dve.tensor_scalar(aux_high[rows, high, :], side[rows, bank, :], add, None, ALU.add).then_inc(aux_rounded, 1)
            dve.wait_ge(aux_rounded, count + 1)
            dve.scalar_tensor_tensor(out, aux_high[rows, high, :].bitcast(F32), keep, side[rows, bank, :],
                                     ALU.mult, ALU.add).then_inc(side_free[bank], 1)

        def keys_rank_four(bank, n, parity, j, rounds):
            rank_four(bank, n, k_high[rows, parity, j * QB:(j + 1) * QB], add_k, keep_k, rounds, 0)

        def queries_rank_four(bank, n, slot, rounds):
            rank_four(bank, n, q_low[rows, slot, :], add_q, keep_q, rounds, 1)

        def gate(bank, n, parity, slot):
            dve.wait_ge(side_full[bank], n + 1)
            dve.tensor_scalar(gates[:, slot, :], side[:, bank, :], head_w[:, parity, OFF_B + 2:OFF_B + 3], None,
                              ALU.add).then_inc(side_free[bank], 1)

        def value(bank, n, parity, j):
            dve.wait_ge(side_full[bank], n + 1)
            bias = head_w[:, parity, OFF_BV:OFF_BV + DH].unsqueeze(1).broadcast_to([P, 4, DH])
            dve.tensor_tensor(values[:, parity, 4 * j:4 * j + 4, :],
                              side[:, bank, 0:4 * DH].rearrange("p (t d) -> p t d", t=4), bias,
                              ALU.add).then_inc(side_free[bank], 1)

        def clip(slot, k, units):
            dve.wait_ge(scored, units + k + 1)
            dve.wait_ge(mixing, units + k + 2)
            dve.wait_ge(summed, units + k + 1)
            dve.tensor_scalar(weights[:, slot * UNITS + k, :], scores[:, k % 2, :], -2.0, 0.0,
                              ALU.mult, ALU.max).then_inc(clipped, 1)

        def denominator(bank, n, slot):
            dve.wait_ge(side_full[bank], n + 1)
            dve.tensor_scalar(den[:, slot, :], side[:, bank, 0:4], EPS, None, ALU.add).then_inc(side_free[bank], 1)
            dve.wait_ge(side_free[bank], n + 1)
            dve.reciprocal(rden[:, slot, :], den[:, slot, :]).then_inc(rden_done, 1)

        def apply_gate(slot, g, step):
            dve.wait_ge(mixing, step * UNITS + 1)
            dve.tensor_tensor(gated[:, slot, :], mixed[:, slot, :], gates[:, g, :], ALU.mult).then_inc(gate_done, 1)

        def add_out(bank, n, slot, j, step):
            dve.wait_ge(side_full[bank], n + 1)
            dve.wait_ge(rden_done, step + 2)
            for i in range(4):
                last = dve.scalar_tensor_tensor(x[:, 4 * j + i, :], side[:, bank, i * P:(i + 1) * P],
                                                rden[:, slot, i:i + 1], x[:, 4 * j + i, :], ALU.mult, ALU.add)
            last.then_inc(side_free[bank], 1)

        dve.memset(mixed[:, 1, :], 0.0).then_inc(clipped, 2)
        dve.memset(primer[:, 2:3], 0.0).then_inc(rden_done, 1)
        dve.memset(primer[:, 3:4], 0.0).then_inc(gate_done, 1)
        dve.memset(primer[:, 5:6], 0.0).then_inc(mixing, 1)
        for j in range(BLOCKS):
            keys(0, j + min(j, 2), 0, j, j)
            if j < BLOCKS - 2:
                value(0, 2 * j + 1, 0, j)
            keys_rank_four(1, j, 0, j, j)
        queries(1, BLOCKS, 0, 0, 0)
        gate(0, BLOCKS + 2, 0, 0)
        queries_rank_four(0, BLOCKS + 3, 0, BLOCKS)
        with dve.Fori(0, TURNS) as turn:
            for b in range(STEPS):
                parity, j = divmod(b, BLOCKS)
                step = turn * STEPS + b
                n0, n1 = turn * (4 * STEPS) + PRE[0] + 4 * b, turn * (4 * STEPS) + PRE[1] + 4 * b
                q_parity = (b + 1) // BLOCKS % 2
                units = turn * (STEPS * UNITS) + b * UNITS
                rounds = turn * (2 * STEPS) + BLOCKS + 1 + 2 * b
                apply_gate((b - 3) % 2, (b - 3) % STEPS, step)
                for k in range(UNITS):
                    clip(b % 2, k, units)
                    if k == 0:
                        keys(0, n0, 1 - parity, j, step + BLOCKS)
                    if k == 1:
                        queries(1, n1, q_parity, (b + 1) % 2, step + 1)
                    if k == 2:
                        gate(0, n0 + 1, q_parity, (b + 1) % STEPS)
                    if k == 3:
                        value(1, n1 + 1, *value_of(b))
                    if k == 4:
                        keys_rank_four(0, n0 + 2, 1 - parity, j, rounds)
                    if k == 5:
                        queries_rank_four(1, n1 + 2, (b + 1) % 2, rounds + 1)
                    if k == 6:
                        denominator(0, n0 + 3, (b - 3) % 2)
                    if k == 7:
                        add_out(1, n1 + 3, (b - 3) % 2, (b - 3) % BLOCKS, step)
        steps = TURNS * STEPS
        n0, n1 = PRE[0] + 4 * steps, PRE[1] + 4 * steps
        for b in range(3):
            apply_gate((b - 3) % 2, (b - 3) % STEPS, steps + b)
            denominator(0, n0 + b, (b - 3) % 2)
            add_out(1, n1 + b, (b - 3) % 2, (b - 3) % BLOCKS, steps + b)


def fp4_feed_forward(nc, ctx, x, xn, gate_in, up_in, down_in, identity):
    def sb(name, shape, dt=F32):
        return ctx.enter_context(nc.sbuf_tensor(f"ff_{name}", shape, dt))

    def ps(name, shape):
        return ctx.enter_context(nc.psum_tensor(f"ff_{name}", shape, F32))

    def sem(name):
        return ctx.enter_context(nc.semaphore(f"ff_{name}"))

    PAIRS = TILES // 2
    TURNS_BEFORE = 3 + BLOCKS
    widest = 2 * INNER
    gate_w = sb("gate_w", [CHUNK, CHUNKS, E])
    up_w = sb("up_w", [CHUNK, CHUNKS, E])
    down_w = sb("down_w", [P, INNER])
    gate_q = sb("gate_q", [CHUNK, CHUNKS, E])
    up_q = sb("up_q", [CHUNK, CHUNKS, E])
    down_q = sb("down_q", [P, INNER])
    gate_t = sb("gate_t", [P, INNER])
    up_t = sb("up_t", [P, INNER])
    down_t = sb("down_t", [CHUNK, CHUNKS, E])
    x_q = sb("x_q", [P, TILES, E])
    x_t = sb("x_t", [P, T])
    silu = sb("silu", [P, 2, INNER])
    hidden = sb("hidden", [P, 2, 2, INNER])
    hidden_q = sb("hidden_q", [P, 2, 2, INNER])
    hidden_t = sb("hidden_t", [CHUNK, 2, 2, QB])
    size = sb("size", [P, 2, widest])
    sign = sb("sign", [P, 2, widest], BF16)
    level = sb("level", [P, 2, widest], BF16)
    scale = sb("scale", [P, 2, widest // FP4_BLOCK])
    inverse = sb("inverse", [P, 2, widest // FP4_BLOCK])
    half_scale = sb("half_scale", [P, 2, widest // FP4_BLOCK])
    turned = ps("turned", [P, 2, QB])
    gated = ps("gated", [P, 2, QB])
    upped = ps("upped", [P, 2, QB])
    downed = ps("downed", [P, 2, QB])

    loaded = sem("loaded")
    sized = sem("sized")
    chain = sem("chain")
    levelled = sem("levelled")
    signed = sem("signed")
    quantised = sem("quantised")
    turned_full = sem("turned_full")
    turned_free = sem("turned_free")
    gate_ready = sem("gate_ready")
    up_ready = sem("up_ready")
    silu_ready = sem("silu_ready")
    hidden_ready = sem("hidden_ready")
    down_ready = sem("down_ready")
    added = sem("added")
    block = ctx.enter_context(nc.Block())

    def flat(t):
        return t.rearrange("p a b -> p (a b)")

    jobs = [(CHUNK, CHUNKS * E, flat(gate_w[:, :, :]), flat(gate_q[:, :, :])),
            (CHUNK, CHUNKS * E, flat(up_w[:, :, :]), flat(up_q[:, :, :])),
            (P, INNER, down_w[:, :], down_q[:, :])]
    for c in range(BLOCKS):
        jobs.append((P, 4 * E, flat(xn[:, 4 * c:4 * c + 4, :]), flat(x_q[:, 4 * c:4 * c + 4, :])))
    FIRST_HIDDEN = len(jobs)
    for i in range(PAIRS):
        jobs.append((P, widest, flat(hidden[:, i % 2, :, :]), flat(hidden_q[:, i % 2, :, :])))

    def source_ready(engine, n):
        if n < FIRST_HIDDEN:
            engine.wait_ge(loaded, 48)
        else:
            engine.wait_ge(hidden_ready, n - FIRST_HIDDEN + 1)

    def blocks(t, parts, slot, width):
        return t[0:parts, slot, 0:width].rearrange("p (b c) -> p b c", c=FP4_BLOCK)

    def spread(t, parts, slot, width):
        n = width // FP4_BLOCK
        return t[0:parts, slot, 0:n].unsqueeze(2).broadcast_to([parts, n, FP4_BLOCK])

    @block.sync
    def _(sp):
        sp.dma_start(gate_w[:, :, :], gate_in.rearrange("(c p) e -> p c e", p=CHUNK)).then_inc(loaded, 16)
        sp.dma_start(up_w[:, :, :], up_in.rearrange("(c p) e -> p c e", p=CHUNK)).then_inc(loaded, 16)
        sp.dma_start(down_w[:, :], down_in).then_inc(loaded, 16)

    @block.vector
    def _(dve):
        steps = 0

        def then(instruction):
            nonlocal steps
            steps += 1
            instruction.then_inc(chain, 1)
            dve.wait_ge(chain, steps)

        def levels(n):
            parts, width, source, _ = jobs[n]
            slot = n % 2
            nb = width // FP4_BLOCK
            source_ready(dve, n)
            if n >= 2:
                dve.wait_ge(quantised, n - 1)
            sc, inv = scale[0:parts, slot, 0:nb], inverse[0:parts, slot, 0:nb]
            then(dve.tensor_reduce(sc, source.rearrange("p (b c) -> p b c", c=FP4_BLOCK), AX.X, ALU.max,
                                   apply_absolute_value=True))
            then(dve.tensor_scalar(sc, sc, 1.0 / 6.0, 1e-12, ALU.mult, ALU.max))
            dve.tensor_scalar(half_scale[0:parts, slot, 0:nb], sc, 0.5, None, ALU.mult)
            then(dve.reciprocal(inv, sc))
            dve.wait_ge(sized, n + 1)
            over = size[0:parts, slot, 0:width]
            then(dve.tensor_tensor(blocks(size, parts, slot, width), blocks(size, parts, slot, width),
                                   spread(inverse, parts, slot, width), ALU.mult))
            out = level[0:parts, slot, 0:width]
            then(dve.tensor_scalar(out, over, FP4_MIDDLES[6], 2.0, ALU.is_gt, ALU.mult))
            then(dve.scalar_tensor_tensor(out, over, FP4_MIDDLES[5], out, ALU.is_gt, ALU.add))
            then(dve.scalar_tensor_tensor(out, over, FP4_MIDDLES[4], out, ALU.is_gt, ALU.add))
            then(dve.tensor_scalar(out, out, 2.0, None, ALU.mult))
            for middle in FP4_MIDDLES[3:0:-1]:
                then(dve.scalar_tensor_tensor(out, over, middle, out, ALU.is_gt, ALU.add))
            dve.scalar_tensor_tensor(out, over, FP4_MIDDLES[0], out, ALU.is_gt, ALU.add).then_inc(levelled, 1)

        for n in range(FIRST_HIDDEN):
            levels(n)
        for i in range(PAIRS + 1):
            if i < PAIRS:
                dve.wait_ge(silu_ready, i + 1)
                dve.wait_ge(up_ready, 2 * i + 2)
                if i >= 2:
                    dve.wait_ge(quantised, FIRST_HIDDEN + i - 1)
                dve.tensor_tensor(hidden[:, i % 2, :, :], silu[:, :, :], upped[:, :, 0:INNER],
                                  ALU.mult).then_inc(hidden_ready, 1)
                levels(FIRST_HIDDEN + i)
            if i >= 1:
                dve.wait_ge(down_ready, i)
                rows = x[:, 2 * (i - 1):2 * i, :]
                dve.tensor_tensor(rows, rows, downed[:, :, 0:E], ALU.add).then_inc(added, 1)

    @block.gpsimd
    def _(pool):
        for n, (parts, width, _, result) in enumerate(jobs):
            slot = n % 2
            pool.wait_ge(levelled, n + 1)
            pool.wait_ge(sized, n + 1)
            if n >= FIRST_HIDDEN + 2:
                pool.wait_ge(turned_full, TURNS_BEFORE + n - FIRST_HIDDEN - 1)
            out = level[0:parts, slot, 0:width]
            pool.tensor_tensor(out, out, sign[0:parts, slot, 0:width], ALU.mult).then_inc(signed, 1)
            pool.wait_ge(signed, n + 1)
            pool.tensor_tensor(result.rearrange("p (b c) -> p b c", c=FP4_BLOCK), blocks(level, parts, slot, width),
                               spread(half_scale, parts, slot, width), ALU.mult).then_inc(quantised, 1)

    @block.scalar
    def _(act):
        def magnitudes(n):
            parts, width, source, _ = jobs[n]
            slot = n % 2
            source_ready(act, n)
            if n >= 2:
                act.wait_ge(quantised, n - 1)
                act.wait_ge(levelled, n - 1)
            act.activation(size[0:parts, slot, 0:width], source, ACT.Abs)
            act.activation(sign[0:parts, slot, 0:width], source, ACT.Sign).then_inc(sized, 1)

        def swish(i):
            act.wait_ge(gate_ready, 2 * i + 2)
            if i >= 1:
                act.wait_ge(hidden_ready, i)
            act.activation(silu[:, :, :], gated[:, :, 0:INNER], ACT.Silu).then_inc(silu_ready, 1)

        for n in range(3):
            magnitudes(n)
        for n, (out, parts, width) in enumerate(((gate_t[:, :], P, INNER), (up_t[:, :], P, INNER),
                                                 (flat(down_t[:, :, :]), CHUNK, QB))):
            magnitudes(n + 3)
            act.wait_ge(turned_full, n + 1)
            act.activation(out, turned[0:parts, n % 2, 0:width], ACT.Copy).then_inc(turned_free, 1)
        magnitudes(6)
        for c in range(BLOCKS):
            act.wait_ge(turned_full, 3 + c + 1)
            act.activation(x_t[:, c * QB:(c + 1) * QB], turned[:, (3 + c) % 2, :], ACT.Copy).then_inc(turned_free, 1)
        swish(0)
        magnitudes(FIRST_HIDDEN)
        for i in range(PAIRS):
            if i + 1 < PAIRS:
                swish(i + 1)
                magnitudes(FIRST_HIDDEN + i + 1)
            act.wait_ge(turned_full, TURNS_BEFORE + i + 1)
            if i >= 2:
                act.wait_ge(down_ready, i - 1)
            act.activation(hidden_t[:, i % 2, :, :], turned[0:CHUNK, :, :], ACT.Copy).then_inc(turned_free, 1)

    @block.tensor
    def _(pe):
        def turn(n, sources, out, parts):
            if n >= 2:
                pe.wait_ge(turned_free, n - 1)
            for i, source in enumerate(sources):
                last = pe.transpose(out(i), source, identity[0:parts, 0:parts])
            last.then_inc(turned_full, 1)

        for n, source in enumerate((gate_q, up_q)):
            pe.wait_ge(quantised, n + 1)
            turn(n, [source[:, c, :] for c in range(CHUNKS)],
                 lambda c, n=n: turned[:, n, c * CHUNK:(c + 1) * CHUNK], CHUNK)
        pe.wait_ge(quantised, 3)
        turn(2, [down_q[:, c * CHUNK:(c + 1) * CHUNK] for c in range(CHUNKS)],
             lambda c: turned[0:CHUNK, 0, c * P:(c + 1) * P], P)
        for b in range(BLOCKS):
            pe.wait_ge(quantised, 3 + b + 1)
            turn(3 + b, [x_q[:, 4 * b + i, :] for i in range(4)],
                 lambda i, b=b: turned[:, (3 + b) % 2, i * P:(i + 1) * P], P)
        for i in range(PAIRS + 1):
            if i < PAIRS:
                for t in range(2):
                    if t == 0:
                        pe.wait_ge(turned_free, 3 + i // 2 + 1)
                        if i >= 1:
                            pe.wait_ge(silu_ready, i)
                    rows = x_t[:, (2 * i + t) * P:(2 * i + t + 1) * P]
                    pe.matmul(gated[:, t, 0:INNER], rows, gate_t[:, :], start=True, stop=True).then_inc(gate_ready, 1)
                for t in range(2):
                    if t == 0 and i >= 1:
                        pe.wait_ge(hidden_ready, i)
                    rows = x_t[:, (2 * i + t) * P:(2 * i + t + 1) * P]
                    pe.matmul(upped[:, t, 0:INNER], rows, up_t[:, :], start=True, stop=True).then_inc(up_ready, 1)
            if i >= 1:
                j = i - 1
                pe.wait_ge(quantised, FIRST_HIDDEN + j + 1)
                pe.wait_ge(turned_free, TURNS_BEFORE + j)
                for t in range(2):
                    for c in range(CHUNKS):
                        last = pe.transpose(turned[0:CHUNK, t, c * P:(c + 1) * P],
                                            hidden_q[:, j % 2, t, c * CHUNK:(c + 1) * CHUNK], identity[:, :])
                last.then_inc(turned_full, 1)
                pe.wait_ge(turned_free, TURNS_BEFORE + j + 1)
                if j >= 1:
                    pe.wait_ge(added, j)
                for t in range(2):
                    for c in range(CHUNKS):
                        last = pe.matmul(downed[:, t, 0:E], hidden_t[:, j % 2, t, c * P:(c + 1) * P],
                                         down_t[:, c, :], start=c == 0, stop=c == CHUNKS - 1)
                last.then_inc(down_ready, 1)


def causal_attention(nc, ctx, x, xnT, heads_in, heads_out, rotary_in, masks_in, table, fold, identity):
    def sb(name, shape, dt=F32):
        return ctx.enter_context(nc.sbuf_tensor(f"ca_{name}", shape, dt))

    def ps(name, shape):
        return ctx.enter_context(nc.psum_tensor(f"ca_{name}", shape, F32))

    def sem(name):
        return ctx.enter_context(nc.semaphore(f"ca_{name}"))

    RING = 4
    SCALE = float(DH) ** -0.5
    head_w = sb("head_w", [P, 2, CW])
    head_o = sb("head_o", [P, 2, E])
    rotary = sb("rotary", [P, T])
    masks_f = sb("masks_f", [P, MASKS])
    masks = sb("masks", [P, MASKS], BF16)
    identity_b = sb("identity_b", [P, P], BF16)
    k_split = sb("k_split", [P, 2, T], F32R)
    k_high = sb("k_high", [P, 2, T], F32R)
    q_high = sb("q_high", [P, 2, QB], F32R)
    q_low = sb("q_low", [P, 2, QB], F32R)
    turned_k = sb("turned_k", [P, QB])
    turned_q = sb("turned_q", [P, QB])
    values = sb("values", [P, 2, TILES, DH])
    weights = sb("weights", [P, RING, 2, QB])
    sums = sb("sums", [P, 2, 2, QB])
    unscaled = sb("unscaled", [P, 2, QB])
    maxima = sb("maxima", [P, 2, 4, 2])
    top = sb("top", [P, 2, 4])
    neg_top = sb("neg_top", [P, 2, 4])
    aux_high = sb("aux_high", [P, 2, QB], F32R)
    rden = sb("rden", [P, 2, 4])
    ones = sb("ones", [P, 1])
    primer = sb("primer", [P, 4])

    scores = ps("scores", [P, 2, 2 * QB])
    mixed = ps("mixed", [P, 2, QB])
    side = ps("side", [P, 2, QB])

    loaded = sem("loaded")
    loaded_w = [sem("loaded_w0"), sem("loaded_w1")]
    loaded_o = [sem("loaded_o0"), sem("loaded_o1")]
    zeroed = sem("zeroed")
    primed = sem("primed")
    cast = sem("cast")
    score_full = [sem("score_full0"), sem("score_full1")]
    score_free = [sem("score_free0"), sem("score_free1")]
    side_full = [sem("side_full0"), sem("side_full1")]
    side_free = [sem("side_free0"), sem("side_free1")]
    rounded = sem("rounded")
    mixing = sem("mixing")
    summed = sem("summed")
    copied = sem("copied")
    top_done = sem("top_done")
    neg_done = sem("neg_done")
    aux_rounded = sem("aux_rounded")
    rden_done = sem("rden_done")
    block = ctx.enter_context(nc.Block())

    TURNS = HEADS // 2
    rows = slice(DH, DH + AUXP)
    keep = table[rows, 68:69]

    def attended(j):
        return 2 * j + 2

    def maxed(j):
        units = []
        for i in range(4):
            tiles = 4 * j + i + 1
            units += [(i, at, min(8, tiles - at)) for at in range(0, tiles, 8)]
        return units

    def order(b):
        n = attended(b % BLOCKS)
        main = [("S", 0), ("S", 1)]
        for u in range(n):
            main.append(("A", u))
            if u + 2 < n:
                main.append(("S", u + 2))
        found = [("X", m) for m in range(len(maxed((b + 1) % BLOCKS)))]
        sides = [(p, 0) for p in ("K1", "Q1", "K2", "Q2", "D", "V")] + found + [("Y", 0), ("M", 0)]
        merged = []
        done = 0
        for i, item in enumerate(sides):
            upto = (i * len(main)) // len(sides)
            merged += main[done:upto] + [item]
            done = upto
        return merged + main[done:]

    SCORE_PRE, SIDE_PRE = len(maxed(0)), 6
    score_at, side_at, unit_at = {}, {}, {}
    for b in range(STEPS):
        for kind, i in order(b):
            if kind in "SX":
                score_at[b, kind, i] = len(score_at)
            if kind in ("K1", "Q1", "K2", "Q2", "Y", "V", "D", "M"):
                side_at[b, kind] = len(side_at)
            if kind == "S":
                unit_at[b, i] = len(unit_at)
    SCORES, SIDES, UNITS_TURN = len(score_at), len(side_at), len(unit_at)
    assert SCORES % 2 == 0 and SIDES % 2 == 0 and SCORE_PRE % 2 == 0 and SIDE_PRE % 2 == 0
    assert UNITS_TURN % RING == 0

    def score_slot(turn, b, kind, i):
        n = SCORE_PRE + score_at[b, kind, i]
        return n % 2, turn * (SCORES // 2) + n // 2

    def side_slot(turn, b, name):
        n = SIDE_PRE + side_at[b, name]
        return n % 2, turn * (SIDES // 2) + n // 2

    def first_column(j, u):
        return 2 * P if 2 * u - 4 * j == 2 else 0

    @block.sync
    def _(sp):
        def load_w(parity, head):
            sp.dma_start(head_w[:, parity, :], heads_in[head]).then_inc(loaded_w[parity], 16)

        def load_o(parity, head):
            sp.dma_start(head_o[:, parity, :], heads_out[head]).then_inc(loaded_o[parity], 16)

        sp.dma_start(rotary[:, :], rotary_in).then_inc(loaded, 16)
        sp.dma_start(masks_f[:, :], masks_in).then_inc(loaded, 16)
        load_w(0, 0)
        load_w(1, 1)
        load_o(0, 0)
        load_o(1, 1)
        with sp.Fori(0, TURNS) as turn:
            last_uses = []
            for b, name in ((0, "Y"), (2, "V"), (4, "Y"), (6, "V")):
                bank, n = side_slot(turn, b, name)
                last_uses.append((side_free[bank], sp.snap(n + 1)))
            sp.wait_ge(*last_uses[0])
            load_o(1, turn * 2 + 1)
            sp.wait_ge(*last_uses[1])
            load_w(0, turn * 2 + 2)
            sp.wait_ge(*last_uses[2])
            load_o(0, turn * 2 + 2)
            sp.wait_ge(*last_uses[3])
            load_w(1, turn * 2 + 3)
        for s in loaded_w + loaded_o:
            sp.wait_ge(s, 16 * (TURNS + 1))

    @block.tensor
    def _(pe):
        def piece(slot):
            bank, n = slot
            if not (isinstance(n, int) and n == 0):
                pe.wait_ge(side_free[bank], n)
            return side[:, bank, :], side_full[bank]

        def rotate(slot, parity, col, j):
            out, full = piece(slot)
            pe.matmul(out, head_w[:, parity, col:col + P], xnT[:, j * QB:(j + 1) * QB],
                      start=True, stop=True).then_inc(full, 1)

        def fold_halves(slot, turned):
            out, full = piece(slot)
            pe.matmul(out, fold[:, :], turned[:, :], start=True, stop=True).then_inc(full, 1)

        def project_v(slot, parity, j):
            out, full = piece(slot)
            for i in range(4):
                t = 4 * j + i
                last = pe.matmul(out[:, i * DH:(i + 1) * DH], xnT[:, t * P:(t + 1) * P],
                                 head_w[:, parity, 2 * P:2 * P + DH], start=True, stop=True)
            last.then_inc(full, 1)

        def find_maxima(bank_count, parity, slot, j, m):
            bank, n = bank_count
            i, at, tiles = maxed(j)[m]
            if not (isinstance(n, int) and n == 0):
                pe.wait_ge(score_free[bank], n)
            for first in range(0, tiles, 4):
                many = min(4, tiles - first)
                diagonal = at + first + many == 4 * j + i + 1
                last = pe.matmul(scores[:, bank, first * P:(first + many) * P], q_high[:, slot, i * P:(i + 1) * P],
                                 k_split[:, parity, (at + first) * P:(at + first + many) * P],
                                 start=True, stop=not diagonal)
                if diagonal:
                    last = pe.matmul(scores[:, bank, (first + many - 1) * P:(first + many) * P], identity_b[:, :],
                                     masks[:, MASK_Q:MASK_Q + P], start=False, stop=True)
            last.then_inc(score_full[bank], 1)

        def spread_maxima(slot, p, count):
            out, full = piece(slot)
            pe.wait_ge(neg_done, count)
            for i in range(4):
                last = pe.matmul(out[rows, i * P:(i + 1) * P], neg_top[:, p, i:i + 1].broadcast_to([P, AUXP]),
                                 identity[:, :], start=True, stop=True)
            last.then_inc(full, 1)

        def score(bank_count, parity, slot, j, u):
            bank, n = bank_count
            pe.wait_ge(score_free[bank], n)
            c0 = first_column(j, u)
            for half in range(2):
                c = 2 * u + half
                r = c - 4 * j
                at = half * QB
                pe.matmul(scores[:, bank, at + c0:at + QB], k_split[:, parity, c * P:(c + 1) * P],
                          q_high[:, slot, c0:QB], start=True, stop=False)
                last = pe.matmul(scores[:, bank, at + c0:at + QB], k_high[0:DH + AUXP, parity, c * P:(c + 1) * P],
                                 q_low[0:DH + AUXP, slot, c0:QB], start=False, stop=r < 0)
                if r >= 0:
                    end = (r + 1) * P
                    last = pe.matmul(scores[:, bank, at + c0:at + end], identity_b[:, :],
                                     masks[:, c0 + MASK_0 - r * P:end + MASK_0 - r * P], start=False, stop=True)
            last.then_inc(score_full[bank], 1)

        def mix(parity, slot, ring, j, u):
            c0 = first_column(j, u)
            for half in range(2):
                last = pe.matmul(mixed[half * DH:(half + 1) * DH, slot, c0:QB], values[:, parity, 2 * u + half, :],
                                 weights[:, ring, half, c0:QB], start=u == 0, stop=u == attended(j) - 1)
            last.then_inc(mixing, 1)

        def total(slot, p):
            out, full = piece(slot)
            for i in range(4):
                for half in range(2):
                    last = pe.matmul(out[:, i:i + 1], sums[:, p, half, i * P:(i + 1) * P], ones[:, :],
                                     start=half == 0, stop=half == 1)
            last.then_inc(full, 1)

        def project_out(slot, p, parity, count):
            out, full = piece(slot)
            pe.wait_ge(copied, count)
            for i in range(4):
                last = pe.matmul(out[:, i * P:(i + 1) * P], unscaled[:, p, i * P:(i + 1) * P],
                                 head_o[:, parity, :], start=True, stop=True)
            last.then_inc(full, 1)

        pe.wait_ge(primed, 1)
        pe.wait_ge(cast, 2)
        pe.wait_ge(loaded_w[0], 16)
        pe.wait_ge(loaded_o[1], 16)
        rotate((0, 0), 0, 0, 0)
        rotate((1, 0), 0, P, 0)
        fold_halves((0, 1), turned_k)
        fold_halves((1, 1), turned_q)
        project_v((0, 2), 0, 0)
        pe.wait_ge(side_free[0], 2)
        pe.wait_ge(side_free[1], 2)
        for m in range(SCORE_PRE):
            find_maxima((m % 2, m // 2), 0, 0, 0, m)
        spread_maxima((1, 2), 0, 1)
        with pe.Fori(0, TURNS) as turn:
            for b in range(STEPS):
                parity, j = divmod(b, BLOCKS)
                step = turn * STEPS + b
                next_parity, next_j = (b + 1) // BLOCKS % 2, (b + 1) % BLOCKS
                for kind, i in order(b):
                    if kind in ("K1", "Q1", "K2", "Q2", "Y", "V", "D", "M"):
                        slot = side_slot(turn, b, kind)
                    if kind == "S":
                        if i == 0:
                            pe.wait_ge(side_free[1], side_slot(turn, b, "Q1")[1])
                        score(score_slot(turn, b, "S", i), parity, b % 2, j, i)
                    elif kind == "A":
                        if i == 0:
                            pe.wait_ge(copied, step + 1)
                        bank, n = score_slot(turn, b, "S", i)
                        pe.wait_ge(score_free[bank], n + 1)
                        mix(parity, b % 2, unit_at[b, i] % RING, j, i)
                    elif kind == "X":
                        if i == 0:
                            for name in ("K2", "Q2"):
                                bank, n = side_slot(turn, b, name)
                                pe.wait_ge(side_free[bank], n + 1)
                        find_maxima(score_slot(turn, b, "X", i), next_parity, (b + 1) % 2, next_j, i)
                    elif kind == "K1":
                        if b == 3 or b == 7:
                            pe.wait_ge(loaded_w[next_parity], turn * 16 + (16 if b == 3 else 32))
                        rotate(slot, next_parity, 0, next_j)
                    elif kind == "Q1":
                        rotate(slot, next_parity, P, next_j)
                    elif kind == "K2":
                        fold_halves(slot, turned_k)
                    elif kind == "Q2":
                        fold_halves(slot, turned_q)
                    elif kind == "V":
                        project_v(slot, next_parity, next_j)
                    elif kind == "M":
                        spread_maxima(slot, (b + 1) % 2, step + 2)
                    elif kind == "D":
                        pe.wait_ge(summed, turn * UNITS_TURN + unit_at[b, 0] + RING)
                        total(slot, (b - 1) % 2)
                    elif kind == "Y":
                        if b % BLOCKS == 1:
                            pe.wait_ge(loaded_o[parity], turn * 16 + 16 + 16 * parity)
                        project_out(slot, (b - 1) % 2, (b - 1) // BLOCKS % 2, step + 2)
        steps = TURNS * STEPS
        n = SIDE_PRE // 2 + TURNS * (SIDES // 2)
        pe.wait_ge(summed, TURNS * UNITS_TURN + RING)
        total((0, n), 1)
        project_out((1, n), 1, 1, steps + 2)

    @block.scalar
    def _(act):
        def high_parts(slot, outs):
            bank, n = slot
            act.wait_ge(side_full[bank], n + 1)
            for out, parts in outs:
                last = act.activation(out, side[0:parts, bank, :], ACT.Copy)
            last.then_inc(rounded, 1)

        def key_outs(parity, j):
            cols = slice(j * QB, (j + 1) * QB)
            return [(k_high[0:DH, parity, cols], DH), (k_split[:, parity, cols], P)]

        def copy_mixed(p, units):
            act.wait_ge(mixing, units)
            act.activation(unscaled[:, p, :], mixed[:, p, :], ACT.Copy).then_inc(copied, 1)

        act.wait_ge(loaded, 32)
        act.activation(masks[:, :], masks_f[:, :], ACT.Copy).then_inc(cast, 1)
        act.activation(identity_b[:, :], identity[:, :], ACT.Copy).then_inc(cast, 1)
        act.wait_ge(primed, 1)
        high_parts((0, 1), key_outs(0, 0))
        high_parts((1, 1), [(q_high[:, 0, :], P)])
        with act.Fori(0, TURNS) as turn:
            for b in range(STEPS):
                parity, j = divmod(b, BLOCKS)
                step = turn * STEPS + b
                next_parity, next_j = (b + 1) // BLOCKS % 2, (b + 1) % BLOCKS
                copy_mixed((b - 1) % 2, turn * UNITS_TURN + unit_at[b, 0] + RING)
                for kind, i in order(b):
                    if kind == "S":
                        bank, n = score_slot(turn, b, "S", i)
                        c0 = first_column(j, i)
                        u = turn * UNITS_TURN + unit_at[b, i]
                        ring = unit_at[b, i] % RING
                        act.wait_ge(score_full[bank], n + 1)
                        act.wait_ge(mixing, u + 1)
                        act.wait_ge(summed, u + 1)
                        act.activation(weights[:, ring, :, c0:QB],
                                       scores[:, bank, :].rearrange("p (a q) -> p a q", a=2)[:, :, c0:QB],
                                       ACT.Exp, scale=SCALE).then_inc(score_free[bank], 1)
                    elif kind == "K2":
                        high_parts(side_slot(turn, b, "K2"), key_outs(next_parity, next_j))
                    elif kind == "Q2":
                        high_parts(side_slot(turn, b, "Q2"), [(q_high[:, (b + 1) % 2, :], P)])
        copy_mixed(1, TURNS * UNITS_TURN + RING)

    @block.gpsimd
    def _(pool):
        pool.memset(ones[:, :], 1.0).then_inc(zeroed, 1)
        pool.wait_ge(zeroed, 1)
        pool.memset(k_high[rows, :, :].bitcast(F32), 0.0).then_inc(zeroed, 1)
        pool.wait_ge(zeroed, 2)
        pool.memset(k_high[DH:DH + 2, :, :].bitcast(F32), 1.0).then_inc(primed, 1)

    @block.vector
    def _(dve):
        def times_rotary(slot, turned, parity, bias, j):
            bank, n = slot
            dve.wait_ge(side_full[bank], n + 1)
            dve.scalar_tensor_tensor(turned[:, :], side[:, bank, :], head_w[:, parity, bias:bias + 1],
                                     rotary[:, j * QB:(j + 1) * QB], ALU.add, ALU.mult).then_inc(side_free[bank], 1)

        def low_parts(slot, part, out, high, count):
            bank, n = slot
            dve.wait_ge(rounded, count)
            dve.tensor_tensor(out, side[part, bank, :], high.bitcast(F32), ALU.subtract).then_inc(side_free[bank], 1)

        def key_low(slot, parity, j, count):
            part = k_split[DH:P, parity, j * QB:(j + 1) * QB]
            low_parts(slot, slice(DH, P), part, part, count)

        def query_low(slot, p, count):
            low_parts(slot, slice(0, DH), q_low[0:DH, p, :], q_high[0:DH, p, :], count)

        def value(slot, parity, j):
            bank, n = slot
            dve.wait_ge(side_full[bank], n + 1)
            bias = head_w[:, parity, CV:CV + DH].unsqueeze(1).broadcast_to([P, 4, DH])
            dve.tensor_tensor(values[:, parity, 4 * j:4 * j + 4, :],
                              side[:, bank, 0:4 * DH].rearrange("p (t d) -> p t d", t=4), bias,
                              ALU.add).then_inc(side_free[bank], 1)

        def maximum(bank_count, p, j, m):
            bank, n = bank_count
            i, at, tiles = maxed(j)[m]
            dve.wait_ge(score_full[bank], n + 1)
            dve.tensor_reduce(maxima[:, p, i, at // 8:at // 8 + 1], scores[:, bank, 0:tiles * P], AX.X,
                              ALU.max).then_inc(score_free[bank], 1)

        def negate_maxima(p, j, last_two, count):
            for bank, n in last_two:
                dve.wait_ge(score_free[bank], n + 1)
            parts = 1 if j < 2 else 2
            dve.tensor_reduce(top[:, p, :], maxima[:, p, :, 0:parts], AX.X, ALU.max).then_inc(top_done, 1)
            dve.wait_ge(top_done, count)
            dve.tensor_scalar(neg_top[:, p, :], top[:, p, :], -1.0, None, ALU.mult).then_inc(neg_done, 1)

        def split_maxima(slot, p, count):
            bank, n = slot
            dve.wait_ge(side_full[bank], n + 1)
            dve.tensor_copy(aux_high[rows, p, :], side[rows, bank, :]).then_inc(aux_rounded, 1)
            dve.wait_ge(aux_rounded, count)
            dve.scalar_tensor_tensor(q_low[rows, p, :], aux_high[rows, p, :].bitcast(F32), keep,
                                     side[rows, bank, :], ALU.mult, ALU.add).then_inc(side_free[bank], 1)

        def denominator(slot, p):
            bank, n = slot
            dve.wait_ge(side_full[bank], n + 1)
            dve.reciprocal(rden[:, p, :], side[:, bank, 0:4]).then_inc(side_free[bank], 1)

        def add_out(slot, p, j):
            bank, n = slot
            dve.wait_ge(side_full[bank], n + 1)
            for i in range(4):
                last = dve.scalar_tensor_tensor(x[:, 4 * j + i, :], side[:, bank, i * P:(i + 1) * P],
                                                rden[:, p, i:i + 1], x[:, 4 * j + i, :], ALU.mult, ALU.add)
            last.then_inc(side_free[bank], 1)

        def add_weights(bank_count, p, ring, j, u, units):
            bank, n = bank_count
            c0 = first_column(j, u)
            dve.wait_ge(score_free[bank], n + 1)
            total, new = sums[:, p, :, c0:QB], weights[:, ring, :, c0:QB]
            if u == 0:
                dve.tensor_copy(total, new).then_inc(summed, 1)
            else:
                dve.wait_ge(summed, units + RING)
                dve.tensor_tensor(total, total, new, ALU.add).then_inc(summed, 1)

        dve.memset(mixed[:, 1, :], 0.0).then_inc(mixing, RING)
        dve.memset(sums[:, 1, :, :], 1.0).then_inc(summed, RING)
        dve.memset(primer[:, 0:1], 0.0).then_inc(copied, 1)
        dve.wait_ge(loaded, 32)
        times_rotary((0, 0), turned_k, 0, CB, 0)
        times_rotary((1, 0), turned_q, 0, CB + 1, 0)
        key_low((0, 1), 0, 0, 1)
        query_low((1, 1), 0, 2)
        value((0, 2), 0, 0)
        for m in range(SCORE_PRE):
            maximum((m % 2, m // 2), 0, 0, m)
        negate_maxima(0, 0, [(m % 2, m // 2) for m in (SCORE_PRE - 2, SCORE_PRE - 1)], 1)
        split_maxima((1, 2), 0, 1)
        with dve.Fori(0, TURNS) as turn:
            for b in range(STEPS):
                parity, j = divmod(b, BLOCKS)
                step = turn * STEPS + b
                next_parity, next_j = (b + 1) // BLOCKS % 2, (b + 1) % BLOCKS
                found = len(maxed(next_j))
                for kind, i in order(b):
                    if kind == "A":
                        add_weights(score_slot(turn, b, "S", i), b % 2, unit_at[b, i] % RING, j, i,
                                    turn * UNITS_TURN + unit_at[b, i])
                    elif kind == "X":
                        maximum(score_slot(turn, b, "X", i), (b + 1) % 2, next_j, i)
                        if i == found - 1:
                            negate_maxima((b + 1) % 2, next_j,
                                          [score_slot(turn, b, "X", m) for m in (found - 2, found - 1)], step + 2)
                    elif kind == "K1":
                        times_rotary(side_slot(turn, b, kind), turned_k, next_parity, CB, next_j)
                    elif kind == "Q1":
                        times_rotary(side_slot(turn, b, kind), turned_q, next_parity, CB + 1, next_j)
                    elif kind == "K2":
                        key_low(side_slot(turn, b, kind), next_parity, next_j, 2 * step + 3)
                    elif kind == "Q2":
                        query_low(side_slot(turn, b, kind), (b + 1) % 2, 2 * step + 4)
                    elif kind == "V":
                        value(side_slot(turn, b, kind), next_parity, next_j)
                    elif kind == "M":
                        split_maxima(side_slot(turn, b, kind), (b + 1) % 2, step + 2)
                    elif kind == "D":
                        denominator(side_slot(turn, b, kind), (b - 1) % 2)
                    elif kind == "Y":
                        add_out(side_slot(turn, b, kind), (b - 1) % 2, (b - 1) % BLOCKS)
        n = SIDE_PRE // 2 + TURNS * (SIDES // 2)
        denominator((0, n), 1)
        dve.wait_ge(side_free[0], n + 1)
        add_out((1, n), 1, BLOCKS - 1)


def fourier_feed_forward(nc, ctx, x, xnT, dft_in, freq_in, bias_row, out):
    def sb(name, shape, dt=F32):
        return ctx.enter_context(nc.sbuf_tensor(f"fo_{name}", shape, dt))

    def sem(name):
        return ctx.enter_context(nc.semaphore(f"fo_{name}"))

    dft = sb("dft", [P, 3, E])
    freq = sb("freq", [P, 2, E])
    parts = sb("parts", [P, 2, E])
    mixer = sb("mixer", [P, E])
    result = sb("result", [P, TILES, E])
    made = ctx.enter_context(nc.psum_tensor("fo_made", [P, QB], F32))
    product = ctx.enter_context(nc.psum_tensor("fo_product", [P, 2, QB], F32))
    loaded, first, split, second, mixer_done = (sem(n) for n in ("loaded", "first", "split", "second", "mixer_done"))
    multiplied, added, biased, stored = (sem(n) for n in ("multiplied", "added", "biased", "stored"))
    block = ctx.enter_context(nc.Block())

    @block.sync
    def _(sp):
        sp.dma_start(dft[:, :, :], dft_in).then_inc(loaded, 16)
        sp.dma_start(freq[:, :, :], freq_in).then_inc(loaded, 16)
        for b in range(BLOCKS):
            sp.wait_ge(added, b + 1)
            sp.dma_start(out[b * QB:(b + 1) * QB, :].rearrange("(t p) e -> p t e", p=P),
                         result[:, 4 * b:4 * b + 4, :]).then_inc(stored, 16)
        sp.wait_ge(stored, 16 * BLOCKS)

    @block.tensor
    def _(pe):
        pe.wait_ge(loaded, 32)
        pe.matmul(made[:, 0:E], freq[:, 0, :], dft[:, 0, :], start=True, stop=False)
        pe.matmul(made[:, 0:E], freq[:, 1, :], dft[:, 1, :], start=False, stop=True)
        pe.matmul(made[:, E:2 * E], freq[:, 1, :], dft[:, 0, :], start=True, stop=False)
        pe.matmul(made[:, E:2 * E], freq[:, 0, :], dft[:, 2, :], start=False, stop=True).then_inc(first, 1)
        pe.wait_ge(split, 1)
        pe.matmul(made[:, 2 * E:3 * E], parts[:, 0, :], dft[:, 0, :], start=True, stop=False)
        pe.matmul(made[:, 2 * E:3 * E], parts[:, 1, :], dft[:, 2, :], start=False, stop=True).then_inc(second, 1)
        pe.wait_ge(mixer_done, 1)
        for b in range(BLOCKS):
            if b >= 2:
                pe.wait_ge(added, b - 1)
            for i in range(4):
                t = 4 * b + i
                last = pe.matmul(product[:, b % 2, i * P:(i + 1) * P], xnT[:, t * P:(t + 1) * P],
                                 mixer[:, :], start=True, stop=True)
            last.then_inc(multiplied, 1)

    @block.scalar
    def _(act):
        act.wait_ge(first, 1)
        act.activation(parts[:, :, :], made[:, 0:2 * E], ACT.Copy).then_inc(split, 1)
        act.wait_ge(second, 1)
        act.activation(mixer[:, :], made[:, 2 * E:3 * E], ACT.Copy, scale=1.0 / E).then_inc(mixer_done, 1)

    @block.vector
    def _(dve):
        for b in range(BLOCKS):
            tiles = slice(4 * b, 4 * b + 4)
            row = bias_row.unsqueeze(1).broadcast_to([P, 4, E])
            dve.tensor_tensor(result[:, tiles, :], x[:, tiles, :], row, ALU.add).then_inc(biased, 1)
        for b in range(BLOCKS):
            tiles = slice(4 * b, 4 * b + 4)
            dve.wait_ge(multiplied, b + 1)
            dve.wait_ge(biased, b + 1)
            dve.tensor_tensor(result[:, tiles, :], result[:, tiles, :],
                              product[:, b % 2, :].rearrange("p (t e) -> p t e", t=4), ALU.add).then_inc(added, 1)



def run(nc, x_in, heads_in, heads_out, table_in, identity_in, rows_in, gate_in, up_in, down_in,
        causal_in, causal_out, rotary_in, masks_in, fold_in, dft_in, freq_in, out):
    with ExitStack() as ctx:
        x = ctx.enter_context(nc.sbuf_tensor("x", [P, TILES, E], F32))
        xnT = ctx.enter_context(nc.sbuf_tensor("xnT", [P, T], F32))
        table = ctx.enter_context(nc.sbuf_tensor("table", [P, TABLE], F32))
        fold = ctx.enter_context(nc.sbuf_tensor("fold", [P, P], F32))
        identity = ctx.enter_context(nc.sbuf_tensor("identity", [P, P], F32))
        bias_rows = ctx.enter_context(nc.sbuf_tensor("bias_rows", [P, 3, E], F32))
        loaded = ctx.enter_context(nc.semaphore("loaded"))
        stored = ctx.enter_context(nc.semaphore("stored"))
        biased = ctx.enter_context(nc.semaphore("biased"))
        with nc.Block() as block:
            @block.sync
            def _(sp):
                sp.dma_start(x[:, :, :], x_in.rearrange("(t p) e -> p t e", p=P)).then_inc(loaded, 16)
                sp.dma_start(identity[:, :], identity_in).then_inc(loaded, 16)
                sp.dma_start(table[:, :], table_in).then_inc(loaded, 16)
                sp.dma_start(bias_rows[:, :, :], rows_in).then_inc(loaded, 16)
                sp.dma_start(fold[:, :], fold_in).then_inc(loaded, 16)
                sp.wait_ge(loaded, 80)

        with ExitStack() as stage:
            layer_norm(nc, stage, x, xnT, identity, "ln0")

        def add_row(n):
            with nc.Block() as block:
                @block.vector
                def _(dve):
                    for t in range(TILES):
                        dve.tensor_tensor(x[:, t, :], x[:, t, :], bias_rows[:, n, :], ALU.add)
        add_row(0)
        with ExitStack() as stage:
            distance_attention(nc, stage, x, xnT, heads_in, heads_out, table, identity)
        with ExitStack() as stage:
            xn = layer_norm(nc, stage, x, None, identity, "ln1")
            fp4_feed_forward(nc, stage, x, xn, gate_in, up_in, down_in, identity)
        with ExitStack() as stage:
            layer_norm(nc, stage, x, xnT, identity, "ln2")
        add_row(1)
        with ExitStack() as stage:
            causal_attention(nc, stage, x, xnT, causal_in, causal_out, rotary_in, masks_in, table, fold, identity)
        with ExitStack() as stage:
            layer_norm(nc, stage, x, xnT, identity, "ln3")
        with ExitStack() as stage:
            fourier_feed_forward(nc, stage, x, xnT, dft_in, freq_in, bias_rows[:, 2, :], out)


def kernel(**inputs):
    from concourse import bacc
    from concourse.bass_utils import run_bass_kernel_spmd

    a = {k: np.asarray(v) for k, v in inputs.items()}
    w = a["L0_attn_W_in"].reshape(E, HEADS, 4, DH).transpose(1, 0, 2, 3)
    b = a["L0_attn_b_in"].reshape(HEADS, 4, DH)
    columns = np.stack([np.concatenate([b[:, i], b[:, i]], axis=1) for i in (0, 1, 3)], axis=2)
    v_rows = np.broadcast_to(b[:, 2][:, None, :], (HEADS, E, DH))
    packed = np.concatenate([w[:, :, 0], w[:, :, 0], w[:, :, 1], w[:, :, 1], w[:, :, 3], w[:, :, 3],
                             w[:, :, 2], columns, v_rows], axis=2)
    wo = a["L0_attn_W_out"].reshape(HEADS, DH, E)
    wo = np.concatenate([wo, wo], axis=1)
    table = np.zeros((P, TABLE), np.float32)
    table[0:DH, 2:4] = 1.0
    table[0:DH, AUXP:AUXP + 2] = 1.0
    table[DH:DH + AUX, 64] = [-0.5, -0.5, 0, 0]
    table[DH:DH + AUX, 65] = [1, 1, 0, -1]
    table[DH:DH + AUX, 66] = [0, 0, -0.5, -0.5]
    table[DH:DH + AUX, 67] = [0, -1, 1, 1]
    table[DH + 1, 68] = -1.0
    def head_rows(n):
        return a[f"L1_attn_{n}"].reshape(HEADS, DH, -1)

    swap = np.arange(DH) ^ 1
    wk, wq, wv = (head_rows(n).transpose(0, 2, 1) for n in ("wk", "wq", "wv"))
    bk, bq = (head_rows(n) for n in ("bk", "bq"))
    bv = np.broadcast_to(a["L1_attn_bv"].reshape(HEADS, 1, DH), (HEADS, E, DH))
    causal = np.concatenate([wk, wk[:, :, swap], wq, wq[:, :, swap], wv,
                             np.concatenate([bk, bk[:, swap]], axis=1), np.concatenate([bq, bq[:, swap]], axis=1),
                             bv], axis=2)
    co = a["L1_attn_wo"].T.reshape(HEADS, DH, E)
    co = np.concatenate([co, co], axis=1)
    theta = np.float32(10000.0) ** (np.arange(0, DH, 2, dtype=np.float32) / np.float32(DH))
    turns = np.arange(T, dtype=np.float32)[None, :] * (np.float32(1.0) / theta)[:, None]
    turns = np.concatenate([turns, turns]).astype(np.float32)
    sign = np.where(np.arange(DH) % 2 == 0, -1.0, 1.0)[:, None]
    rotary = np.concatenate([np.cos(turns), np.sin(turns) * sign]).astype(np.float32)
    masks = np.zeros((P, MASKS), np.float32)
    p = np.arange(P)[:, None]
    masks[:, :MASK_Q] = np.where(np.arange(MASK_Q)[None, :] - MASK_0 < p, -1e30, 0.0)
    masks[:, MASK_Q:] = np.where(np.arange(P)[None, :] > p, -1e30, 0.0)
    angle = 2.0 * np.pi * np.outer(np.arange(E), np.arange(E)) / E
    dft = np.stack([np.cos(angle), np.sin(angle), -np.sin(angle)], axis=1).astype(np.float32)
    rows = np.stack([np.broadcast_to(a[n], (P, E)) for n in ("L0_attn_b_out", "L1_attn_bo", "L1_ffn_bias")], axis=1)
    arrays = {
        "x": a["L0_attn_X"].reshape(T, E),
        "heads_in": np.concatenate([packed, packed[:2]]),
        "heads_out": np.concatenate([wo, wo[:2]]),
        "table": table,
        "identity": np.eye(P, dtype=np.float32),
        "rows": rows,
        "gate": a["L0_ffn_w_gate"],
        "up": a["L0_ffn_w_up"],
        "down": a["L0_ffn_w_down"],
        "causal": np.concatenate([causal, causal[:2]]),
        "causal_out": np.concatenate([co, co[:2]]),
        "rotary": rotary,
        "masks": masks,
        "fold": (np.arange(P)[:, None] % DH == np.arange(P)[None, :] % DH).astype(np.float32),
        "dft": dft,
        "freq": np.stack([a["L1_ffn_w_freq_real"], a["L1_ffn_w_freq_imag"]], axis=1),
    }
    arrays = {f"in_{k}": np.ascontiguousarray(v) for k, v in arrays.items()}
    nc = bacc.Bacc("TRN2", target_bir_lowering=False, num_devices=1)
    aps = [nc.dram_tensor(k, v.shape, mybir.dt.from_np(v.dtype), kind="ExternalInput").ap() for k, v in arrays.items()]
    out = nc.dram_tensor("out", (T, E), F32, kind="ExternalOutput").ap()
    run(nc, *aps, out)
    result = run_bass_kernel_spmd(nc, [arrays], core_ids=[0])
    return result.results[0]["out"].reshape(1, T, E)
```

```python
import numpy as np

import concourse.bass as bass
from concourse import mybir
from contextlib import ExitStack

F32 = mybir.dt.float32
F32R = mybir.dt.float32r
BF16 = mybir.dt.bfloat16
ALU = mybir.AluOpType
ACT = mybir.ActivationFunctionType
AX = mybir.AxisListType

P = 128
T = 2048
E = 128
HEADS = 16
DH = 64
TILES = T // P
QB = 512
BLOCKS = T // QB
LN_EPS = 1e-5
UNITS = TILES // 2
STEPS = 2 * BLOCKS
PW = 7 * DH + 3 + DH
OFF_K, OFF_G, OFF_V, OFF_B, OFF_BV = 2 * DH, 4 * DH, 6 * DH, 7 * DH, 7 * DH + 3
AUX = 4
AUXP = 32
INNER = 352
CHUNKS = 4
CHUNK = INNER // CHUNKS
FP4_BLOCK = 16
FP4_MIDDLES = (0.25, 0.75, 1.25, 1.75, 2.5, 3.5, 5.0)
CW = 2 * P + DH + 2 + DH
CB, CV = 2 * P + DH, 2 * P + DH + 2
MASK_0 = QB - P
MASK_Q = MASK_0 + QB
MASKS = MASK_Q + P
TABLE = 69
LOG_EXP_SET = "natural_log_exp_and_others"


def layer_norm(nc, ctx, x, xnT, identity, name):
    xn = ctx.enter_context(nc.sbuf_tensor(f"{name}_xn", [P, TILES, E], F32))
    stats = ctx.enter_context(nc.sbuf_tensor(f"{name}_stats", [P, TILES, 6], F32))
    moments = ctx.enter_context(nc.sbuf_tensor(f"{name}_moments", [P, TILES, 2], F32))
    std = ctx.enter_context(nc.sbuf_tensor(f"{name}_std", [P, TILES], F32))
    rstd = ctx.enter_context(nc.sbuf_tensor(f"{name}_rstd", [P, TILES], F32))
    eps = ctx.enter_context(nc.sbuf_tensor(f"{name}_eps", [P, 1], F32))
    if xnT is not None:
        flipped = ctx.enter_context(nc.psum_tensor(f"{name}_flipped", [P, 2, QB], F32))
    have_stats = ctx.enter_context(nc.semaphore(f"{name}_have_stats"))
    have_moments = ctx.enter_context(nc.semaphore(f"{name}_have_moments"))
    have_std = ctx.enter_context(nc.semaphore(f"{name}_have_std"))
    have_rstd = ctx.enter_context(nc.semaphore(f"{name}_have_rstd"))
    have_rows = ctx.enter_context(nc.semaphore(f"{name}_have_rows"))
    have_flipped = ctx.enter_context(nc.semaphore(f"{name}_have_flipped"))
    copied = ctx.enter_context(nc.semaphore(f"{name}_copied"))
    with nc.Block() as block:
        @block.vector
        def _(dve):
            dve.memset(eps[:, :], LN_EPS)
            for t in range(TILES):
                dve.bn_stats(stats[:, t, :], x[:, t, :]).then_inc(have_stats, 1)
            for t in range(TILES):
                dve.wait_ge(have_stats, t + 1)
                dve.bn_aggr(moments[:, t, :], stats[:, t, :]).then_inc(have_moments, 1)
            dve.wait_ge(have_std, 1)
            dve.reciprocal(rstd[:, :], std[:, :]).then_inc(have_rstd, 1)
            dve.wait_ge(have_rstd, 1)
            for t in range(TILES):
                dve.tensor_scalar(xn[:, t, :], x[:, t, :], moments[:, t, 0:1], rstd[:, t:t + 1],
                                  ALU.subtract, ALU.mult).then_inc(have_rows, 1)

        @block.scalar
        def _(act):
            act.wait_ge(have_moments, TILES)
            act.activation(std[:, :], moments[:, :, 1], ACT.Sqrt, bias=eps[:, 0:1]).then_inc(have_std, 1)
            if xnT is not None:
                for b in range(BLOCKS):
                    act.wait_ge(have_flipped, 4 * b + 4)
                    act.activation(xnT[:, b * QB:(b + 1) * QB], flipped[:, b % 2, :], ACT.Copy).then_inc(copied, 1)

        if xnT is not None:
            @block.tensor
            def _(pe):
                for t in range(TILES):
                    b = t // 4
                    if t % 4 == 0 and b >= 2:
                        pe.wait_ge(copied, b - 1)
                    pe.wait_ge(have_rows, t + 1)
                    pe.transpose(flipped[:, b % 2, (t % 4) * P:(t % 4 + 1) * P], xn[:, t, :],
                                 identity[:, :]).then_inc(have_flipped, 1)
    return xn


def distance_attention(nc, ctx, x, xnT, heads_in, heads_out, table):
    def sb(name, shape, dt=F32):
        return ctx.enter_context(nc.sbuf_tensor(f"da_{name}", shape, dt))

    def ps(name, shape):
        return ctx.enter_context(nc.psum_tensor(f"da_{name}", shape, F32))

    def sem(name):
        return ctx.enter_context(nc.semaphore(f"da_{name}"))

    EPS = 1e-4
    head_w = sb("head_w", [P, 2, PW])
    head_o = sb("head_o", [P, 2, E])
    k_split = sb("k_split", [P, 2, T], F32R)
    k_high = sb("k_high", [P, 2, T], F32R)
    q_high = sb("q_high", [P, 2, QB], F32R)
    q_low = sb("q_low", [P, 2, QB], F32R)
    values = sb("values", [P, 2, TILES, DH])
    gates = sb("gates", [P, STEPS, QB])
    weights = sb("weights", [P, 2 * UNITS, 2 * QB])
    sums = sb("sums", [P, 2, 2 * QB])
    gated = sb("gated", [P, 2, QB])
    k_full = sb("k_full", [P, QB])
    q_full = sb("q_full", [P, QB])
    k_square = sb("k_square", [P, QB])
    q_square = sb("q_square", [P, QB])
    aux_high = sb("aux_high", [P, 2, QB], F32R)
    den = sb("den", [P, 2, 4])
    rden = sb("rden", [P, 2, 4])
    ones = sb("ones", [P, 1])
    primer = sb("primer", [P, 6])
    eps = sb("eps", [P, 1])

    scores = ps("scores", [P, 2, 2 * QB])
    mixed = ps("mixed", [P, 2, QB])
    side = ps("side", [P, 2, QB])

    loaded_w = [sem("loaded_w0"), sem("loaded_w1")]
    loaded_o = [sem("loaded_o0"), sem("loaded_o1")]
    primed = sem("primed")
    scored = sem("scored")
    clipped = sem("clipped")
    rooted = sem("rooted")
    logged = sem("logged")
    weighed = sem("weighed")
    mixing = sem("mixing")
    summed = sem("summed")
    folded = sem("folded")
    side_full = [sem("side_full0"), sem("side_full1")]
    side_free = [sem("side_free0"), sem("side_free1")]
    k_copied = sem("k_copied")
    q_copied = sem("q_copied")
    k_squared = sem("k_squared")
    q_squared = sem("q_squared")
    k_rounded = sem("k_rounded")
    q_rounded = sem("q_rounded")
    aux_rounded = sem("aux_rounded")
    rden_done = sem("rden_done")
    gate_done = sem("gate_done")
    block = ctx.enter_context(nc.Block())

    sel_k, sel_q = table[:, 0:AUXP], table[:, AUXP:2 * AUXP]
    rows = slice(DH, DH + AUXP)
    add_k, keep_k = table[rows, 64:65], table[rows, 65:66]
    add_q, keep_q = table[rows, 66:67], table[rows, 67:68]
    TURNS = HEADS // 2
    PRE = [2 * BLOCKS, BLOCKS + 1]

    def value_of(b):
        parity, j = divmod(b, BLOCKS)
        return (parity, j + BLOCKS - 2) if j < 2 else (1 - parity, j - 2)


    @block.sync
    def _(sp):
        def load_w(parity, head):
            sp.dma_start(head_w[:, parity, :], heads_in[head]).then_inc(loaded_w[parity], 16)

        def load_o(parity, head):
            sp.dma_start(head_o[:, parity, :], heads_out[head]).then_inc(loaded_o[parity], 16)

        load_w(0, 0)
        load_w(1, 1)
        load_o(0, 0)
        load_o(1, 1)
        with sp.Fori(0, TURNS) as turn:
            first_out = sp.snap(turn * (4 * STEPS) + PRE[1] + 4 * 2 + 4)
            first_in = sp.snap(turn * (4 * STEPS) + PRE[0] + 4 * 2 + 2)
            second_out = sp.snap(turn * (4 * STEPS) + PRE[1] + 4 * 6 + 4)
            second_in = sp.snap(turn * (4 * STEPS) + PRE[0] + 4 * 6 + 2)
            sp.wait_ge(side_free[0], first_in)
            load_w(0, turn * 2 + 2)
            sp.wait_ge(side_free[1], first_out)
            load_o(1, turn * 2 + 1)
            sp.wait_ge(side_free[1], second_out)
            load_o(0, turn * 2 + 2)
            sp.wait_ge(side_free[0], second_in)
            load_w(1, turn * 2 + 3)
        for s in loaded_w:
            sp.wait_ge(s, 16 * (TURNS + 1))
        for s in loaded_o:
            sp.wait_ge(s, 16 * (TURNS + 1))

    @block.tensor
    def _(pe):
        def piece(bank, n):
            pe.wait_ge(side_free[bank], n)
            return side[:, bank, :]

        def project(bank, n, parity, col, j):
            pe.matmul(piece(bank, n), head_w[:, parity, col:col + P], xnT[:, j * QB:(j + 1) * QB],
                      start=True, stop=True).then_inc(side_full[bank], 1)

        def project_v(bank, n, parity, j):
            out = piece(bank, n)
            for i in range(4):
                t = 4 * j + i
                last = pe.matmul(out[:, i * DH:(i + 1) * DH], xnT[:, t * P:(t + 1) * P],
                                 head_w[:, parity, OFF_V:OFF_V + DH], start=True, stop=True)
            last.then_inc(side_full[bank], 1)

        def norms(bank, n, sel, square):
            out = piece(bank, n)
            pe.matmul(out[rows, :], sel, square[:, :], start=True, stop=True).then_inc(side_full[bank], 1)

        def total(bank, n, slot):
            out = piece(bank, n)
            for i in range(4):
                last = pe.matmul(out[:, i:i + 1], sums[:, slot, i * P:(i + 1) * P], ones[:, :],
                                 start=True, stop=True)
            last.then_inc(side_full[bank], 1)

        def project_out(bank, n, slot, parity):
            out = piece(bank, n)
            for i in range(4):
                last = pe.matmul(out[:, i * P:(i + 1) * P], gated[:, slot, i * P:(i + 1) * P],
                                 head_o[:, parity, :], start=True, stop=True)
            last.then_inc(side_full[bank], 1)

        def distances(parity, slot, k):
            for half in range(2):
                c = 2 * k + half
                out = scores[:, k % 2, half * QB:(half + 1) * QB]
                pe.matmul(out, k_split[:, parity, c * P:(c + 1) * P], q_high[:, slot, :],
                          start=True, stop=False)
                last = pe.matmul(out, k_high[0:DH + AUXP, parity, c * P:(c + 1) * P],
                                 q_low[0:DH + AUXP, slot, :], start=False, stop=True)
            last.then_inc(scored, 1)

        def mix(parity, slot, k):
            for half in range(2):
                last = pe.matmul(mixed[half * DH:(half + 1) * DH, slot, :],
                                 values[:, parity, 2 * k + half, :],
                                 weights[:, slot * UNITS + k, half * QB:(half + 1) * QB],
                                 start=k == 0, stop=k == UNITS - 1)
            last.then_inc(mixing, 1)

        pe.wait_ge(primed, 1)
        pe.wait_ge(loaded_w[0], 16)
        pe.wait_ge(loaded_o[1], 16)
        for j in range(BLOCKS):
            if j == 0:
                pe.matmul(side[:, 0, :], head_w[:, 0, OFF_K:OFF_K + P], xnT[:, 0:QB],
                          start=True, stop=True).then_inc(side_full[0], 1)
            else:
                project(0, j + min(j, 2), 0, OFF_K, j)
            if j < BLOCKS - 2:
                project_v(0, 2 * j + 1, 0, j)
            pe.wait_ge(k_squared, j + 1)
            if j == 0:
                pe.matmul(side[rows, 1, :], sel_k, k_square[:, :], start=True, stop=True).then_inc(side_full[1], 1)
            else:
                norms(1, j, sel_k, k_square)
        project(1, BLOCKS, 0, 0, 0)
        project(0, BLOCKS + 2, 0, OFF_G, 0)
        pe.wait_ge(q_squared, 1)
        norms(0, BLOCKS + 3, sel_q, q_square)

        with pe.Fori(0, TURNS) as turn:
            for b in range(STEPS):
                parity, j = divmod(b, BLOCKS)
                step = turn * STEPS + b
                n0, n1 = turn * (4 * STEPS) + PRE[0] + 4 * b, turn * (4 * STEPS) + PRE[1] + 4 * b
                q_parity, qj = (b + 1) // BLOCKS % 2, (b + 1) % BLOCKS
                for k in range(UNITS):
                    if k == 0:
                        pe.wait_ge(side_free[0], n0)
                    pe.wait_ge(clipped, turn * (STEPS * UNITS) + b * UNITS + k + 1)
                    distances(parity, b % 2, k)
                    if k == 0:
                        pe.wait_ge(gate_done, step + 1)
                        if b % BLOCKS == 2:
                            pe.wait_ge(side_free[1], n1 - 2)
                    if k % 2 == 0:
                        pe.wait_ge(weighed, turn * (STEPS * BLOCKS) + b * BLOCKS + k // 2 + 1)
                    mix((b - 2) // BLOCKS % 2, b % 2, k)
                    if k == 0:
                        if j == 0:
                            pe.wait_ge(loaded_w[1 - parity], turn * 16 + 16 + 16 * parity)
                        project(0, n0, 1 - parity, OFF_K, j)
                    if k == 1:
                        project(1, n1, q_parity, 0, qj)
                    if k == 2:
                        project(0, n0 + 1, q_parity, OFF_G, qj)
                    if k == 3:
                        project_v(1, n1 + 1, *value_of(b))
                    if k == 4:
                        pe.wait_ge(k_squared, step + BLOCKS + 1)
                        norms(0, n0 + 2, sel_k, k_square)
                    if k == 5:
                        pe.wait_ge(q_squared, step + 2)
                        norms(1, n1 + 2, sel_q, q_square)
                    if k == 6:
                        pe.wait_ge(folded, step + 1)
                        total(0, n0 + 3, (b - 3) % 2)
                    if k == 7:
                        pe.wait_ge(gate_done, step + 2)
                        if b % BLOCKS == 3:
                            pe.wait_ge(loaded_o[parity], turn * 16 + 16 + 16 * parity)
                        project_out(1, n1 + 3, (b - 3) % 2, (b - 3) // BLOCKS % 2)

        steps = TURNS * STEPS
        for b in range(3):
            step, n0, n1 = steps + b, PRE[0] + 4 * steps + b, PRE[1] + 4 * steps + b
            if b < 2:
                pe.wait_ge(gate_done, step + 1)
                for k in range(UNITS):
                    if k % 2 == 0:
                        pe.wait_ge(weighed, step * BLOCKS + k // 2 + 1)
                    mix(1, b, k)
            pe.wait_ge(folded, step + 1)
            total(0, n0, (b - 3) % 2)
            pe.wait_ge(gate_done, step + 2)
            project_out(1, n1, (b - 3) % 2, 1)

    @block.scalar
    def _(act):
        act.wait_ge(primed, 1)
        with act.Fori(0, TURNS) as turn:
            for b in range(STEPS):
                step = turn * STEPS + b
                whole = weights[:, (b % 2) * UNITS:(b % 2 + 1) * UNITS, :]
                halves = [whole[:, 0:UNITS // 2, :], whole[:, UNITS // 2:UNITS, :]]
                for i, w in enumerate(halves):
                    act.wait_ge(clipped, step * UNITS + (i + 1) * (UNITS // 2) + 2)
                    act.activation(w, w, ACT.Sqrt).then_inc(rooted, 1)
                act.preload_act_table_set(LOG_EXP_SET)
                act.wait_ge(rooted, 2 * step + 2)
                act.activation(whole, whole, ACT.Ln, bias=eps[:, 0:1]).then_inc(logged, 1)
                act.wait_ge(logged, step + 1)
                for w in halves:
                    act.activation(w, w, ACT.Exp, scale=-2.0).then_inc(weighed, UNITS // 4)

    @block.gpsimd
    def _(pool):
        def sum_block(slot, n, pairs, units):
            total = sums[:, slot, :]
            for k in range(1, UNITS):
                if k == 1 or k % 2 == 0:
                    pool.wait_ge(weighed, pairs + k // 2 + 1)
                if k == 1:
                    pool.wait_ge(rden_done, n)
                    pool.tensor_tensor(total, weights[:, slot * UNITS, :], weights[:, slot * UNITS + 1, :],
                                       ALU.add).then_inc(summed, 2)
                else:
                    pool.wait_ge(summed, units + k)
                    pool.tensor_tensor(total, total, weights[:, slot * UNITS + k, :],
                                       ALU.add).then_inc(summed, 1)
            pool.wait_ge(summed, units + UNITS)
            pool.tensor_tensor(total[:, 0:QB], total[:, 0:QB], total[:, QB:2 * QB], ALU.add).then_inc(folded, 1)

        pool.memset(values[:, 1, :, :], 0.0)
        pool.memset(gates[:, STEPS - 3:STEPS, :], 0.0)
        pool.memset(sums[:, :, :], 0.0).then_inc(folded, 2)
        pool.memset(ones[:, :], 1.0)
        pool.memset(eps[:, :], EPS)
        pool.memset(primer[:, 4:5], 0.0).then_inc(primed, 1)
        pool.memset(primer[:, 1:2], 0.0).then_inc(summed, UNITS)
        pool.memset(weights[:, :, :], 0.0).then_inc(weighed, UNITS)
        with pool.Fori(0, TURNS) as turn:
            for b in range(STEPS):
                step = turn * STEPS + b
                sum_block((b - 1) % 2, step + 2, turn * (STEPS * BLOCKS) + (b + 1) * BLOCKS,
                          turn * (STEPS * UNITS) + b * UNITS + UNITS)
        steps = TURNS * STEPS
        sum_block(1, steps + 2, (steps + 1) * BLOCKS, steps * UNITS + UNITS)

    @block.vector
    def _(dve):
        def projected(full, bank, n, bias, copied):
            dve.wait_ge(side_full[bank], n + 1)
            dve.tensor_scalar(full[:, :], side[:, bank, :], bias, None, ALU.add).then_inc(copied, 1)

        def keys(bank, n, parity, j, count):
            cols = slice(j * QB, (j + 1) * QB)
            projected(k_full, bank, n, head_w[:, parity, OFF_B + 1:OFF_B + 2], k_copied)
            dve.wait_ge(k_copied, count + 1)
            dve.tensor_copy(k_split[:, parity, cols], k_full[:, :]).then_inc(k_rounded, 1)
            dve.tensor_tensor(k_square[:, :], k_full[:, :], k_full[:, :], ALU.mult).then_inc(k_squared, 1)
            dve.tensor_copy(k_high[0:DH, parity, cols], k_full[0:DH, :]).then_inc(side_free[bank], 1)
            dve.wait_ge(k_rounded, count + 1)
            dve.tensor_tensor(k_split[DH:P, parity, cols], k_full[DH:P, :],
                              k_split[DH:P, parity, cols].bitcast(F32), ALU.subtract)

        def queries(bank, n, parity, slot, count):
            projected(q_full, bank, n, head_w[:, parity, OFF_B:OFF_B + 1], q_copied)
            dve.wait_ge(q_copied, count + 1)
            dve.tensor_copy(q_high[:, slot, :], q_full[:, :]).then_inc(q_rounded, 1)
            dve.tensor_tensor(q_square[:, :], q_full[:, :], q_full[:, :], ALU.mult).then_inc(q_squared, 1)
            dve.wait_ge(q_rounded, count + 1)
            dve.tensor_tensor(q_low[0:DH, slot, :], q_full[0:DH, :], q_high[0:DH, slot, :].bitcast(F32),
                              ALU.subtract).then_inc(side_free[bank], 1)

        def rank_four(bank, n, out, add, keep, count, high):
            dve.wait_ge(side_full[bank], n + 1)
            dve.tensor_scalar(aux_high[rows, high, :], side[rows, bank, :], add, None, ALU.add).then_inc(aux_rounded, 1)
            dve.wait_ge(aux_rounded, count + 1)
            dve.scalar_tensor_tensor(out, aux_high[rows, high, :].bitcast(F32), keep, side[rows, bank, :],
                                     ALU.mult, ALU.add).then_inc(side_free[bank], 1)

        def keys_rank_four(bank, n, parity, j, rounds):
            rank_four(bank, n, k_high[rows, parity, j * QB:(j + 1) * QB], add_k, keep_k, rounds, 0)

        def queries_rank_four(bank, n, slot, rounds):
            rank_four(bank, n, q_low[rows, slot, :], add_q, keep_q, rounds, 1)

        def gate(bank, n, parity, slot):
            dve.wait_ge(side_full[bank], n + 1)
            dve.tensor_scalar(gates[:, slot, :], side[:, bank, :], head_w[:, parity, OFF_B + 2:OFF_B + 3], None,
                              ALU.add).then_inc(side_free[bank], 1)

        def value(bank, n, parity, j):
            dve.wait_ge(side_full[bank], n + 1)
            bias = head_w[:, parity, OFF_BV:OFF_BV + DH].unsqueeze(1).broadcast_to([P, 4, DH])
            dve.tensor_tensor(values[:, parity, 4 * j:4 * j + 4, :],
                              side[:, bank, 0:4 * DH].rearrange("p (t d) -> p t d", t=4), bias,
                              ALU.add).then_inc(side_free[bank], 1)

        def clip(slot, k, units):
            dve.wait_ge(scored, units + k + 1)
            dve.wait_ge(mixing, units + k + 2)
            dve.wait_ge(summed, units + k + 1)
            dve.tensor_scalar(weights[:, slot * UNITS + k, :], scores[:, k % 2, :], -2.0, 0.0,
                              ALU.mult, ALU.max).then_inc(clipped, 1)

        def denominator(bank, n, slot):
            dve.wait_ge(side_full[bank], n + 1)
            dve.tensor_scalar(den[:, slot, :], side[:, bank, 0:4], EPS, None, ALU.add).then_inc(side_free[bank], 1)
            dve.wait_ge(side_free[bank], n + 1)
            dve.reciprocal(rden[:, slot, :], den[:, slot, :]).then_inc(rden_done, 1)

        def apply_gate(slot, g, step):
            dve.wait_ge(mixing, step * UNITS + 1)
            dve.tensor_tensor(gated[:, slot, :], mixed[:, slot, :], gates[:, g, :], ALU.mult).then_inc(gate_done, 1)

        def add_out(bank, n, slot, j, step):
            dve.wait_ge(side_full[bank], n + 1)
            dve.wait_ge(rden_done, step + 2)
            for i in range(4):
                last = dve.scalar_tensor_tensor(x[:, 4 * j + i, :], side[:, bank, i * P:(i + 1) * P],
                                                rden[:, slot, i:i + 1], x[:, 4 * j + i, :], ALU.mult, ALU.add)
            last.then_inc(side_free[bank], 1)

        dve.memset(mixed[:, 1, :], 0.0).then_inc(clipped, 2)
        dve.memset(primer[:, 2:3], 0.0).then_inc(rden_done, 1)
        dve.memset(primer[:, 3:4], 0.0).then_inc(gate_done, 1)
        dve.memset(primer[:, 5:6], 0.0).then_inc(mixing, 1)
        for j in range(BLOCKS):
            keys(0, j + min(j, 2), 0, j, j)
            if j < BLOCKS - 2:
                value(0, 2 * j + 1, 0, j)
            keys_rank_four(1, j, 0, j, j)
        queries(1, BLOCKS, 0, 0, 0)
        gate(0, BLOCKS + 2, 0, 0)
        queries_rank_four(0, BLOCKS + 3, 0, BLOCKS)
        with dve.Fori(0, TURNS) as turn:
            for b in range(STEPS):
                parity, j = divmod(b, BLOCKS)
                step = turn * STEPS + b
                n0, n1 = turn * (4 * STEPS) + PRE[0] + 4 * b, turn * (4 * STEPS) + PRE[1] + 4 * b
                q_parity = (b + 1) // BLOCKS % 2
                units = turn * (STEPS * UNITS) + b * UNITS
                rounds = turn * (2 * STEPS) + BLOCKS + 1 + 2 * b
                apply_gate((b - 3) % 2, (b - 3) % STEPS, step)
                for k in range(UNITS):
                    clip(b % 2, k, units)
                    if k == 0:
                        keys(0, n0, 1 - parity, j, step + BLOCKS)
                    if k == 1:
                        queries(1, n1, q_parity, (b + 1) % 2, step + 1)
                    if k == 2:
                        gate(0, n0 + 1, q_parity, (b + 1) % STEPS)
                    if k == 3:
                        value(1, n1 + 1, *value_of(b))
                    if k == 4:
                        keys_rank_four(0, n0 + 2, 1 - parity, j, rounds)
                    if k == 5:
                        queries_rank_four(1, n1 + 2, (b + 1) % 2, rounds + 1)
                    if k == 6:
                        denominator(0, n0 + 3, (b - 3) % 2)
                    if k == 7:
                        add_out(1, n1 + 3, (b - 3) % 2, (b - 3) % BLOCKS, step)
        steps = TURNS * STEPS
        n0, n1 = PRE[0] + 4 * steps, PRE[1] + 4 * steps
        for b in range(3):
            apply_gate((b - 3) % 2, (b - 3) % STEPS, steps + b)
            denominator(0, n0 + b, (b - 3) % 2)
            add_out(1, n1 + b, (b - 3) % 2, (b - 3) % BLOCKS, steps + b)


def fp4_feed_forward(nc, ctx, x, xn, gate_in, up_in, down_in, identity):
    def sb(name, shape, dt=F32):
        return ctx.enter_context(nc.sbuf_tensor(f"ff_{name}", shape, dt))

    def ps(name, shape):
        return ctx.enter_context(nc.psum_tensor(f"ff_{name}", shape, F32))

    def sem(name):
        return ctx.enter_context(nc.semaphore(f"ff_{name}"))

    PAIRS = TILES // 2
    TURNS_BEFORE = 3 + BLOCKS
    widest = 2 * INNER
    gate_w = sb("gate_w", [CHUNK, CHUNKS, E])
    up_w = sb("up_w", [CHUNK, CHUNKS, E])
    down_w = sb("down_w", [P, INNER])
    gate_q = sb("gate_q", [CHUNK, CHUNKS, E])
    up_q = sb("up_q", [CHUNK, CHUNKS, E])
    down_q = sb("down_q", [P, INNER])
    gate_t = sb("gate_t", [P, INNER])
    up_t = sb("up_t", [P, INNER])
    down_t = sb("down_t", [CHUNK, CHUNKS, E])
    x_q = sb("x_q", [P, TILES, E])
    x_t = sb("x_t", [P, T])
    silu = sb("silu", [P, 2, INNER])
    hidden = sb("hidden", [P, 2, 2, INNER])
    hidden_q = sb("hidden_q", [P, 2, 2, INNER])
    hidden_t = sb("hidden_t", [CHUNK, 2, 2, QB])
    size = sb("size", [P, 2, widest])
    sign = sb("sign", [P, 2, widest], BF16)
    level = sb("level", [P, 2, widest], BF16)
    scale = sb("scale", [P, 2, widest // FP4_BLOCK])
    inverse = sb("inverse", [P, 2, widest // FP4_BLOCK])
    half_scale = sb("half_scale", [P, 2, widest // FP4_BLOCK])
    turned = ps("turned", [P, 2, QB])
    gated = ps("gated", [P, 2, QB])
    upped = ps("upped", [P, 2, QB])
    downed = ps("downed", [P, 2, QB])

    loaded = sem("loaded")
    sized = sem("sized")
    chain = sem("chain")
    levelled = sem("levelled")
    signed = sem("signed")
    quantised = sem("quantised")
    turned_full = sem("turned_full")
    turned_free = sem("turned_free")
    gate_ready = sem("gate_ready")
    up_ready = sem("up_ready")
    silu_ready = sem("silu_ready")
    hidden_ready = sem("hidden_ready")
    down_ready = sem("down_ready")
    added = sem("added")
    block = ctx.enter_context(nc.Block())

    def flat(t):
        return t.rearrange("p a b -> p (a b)")

    jobs = [(CHUNK, CHUNKS * E, flat(gate_w[:, :, :]), flat(gate_q[:, :, :])),
            (CHUNK, CHUNKS * E, flat(up_w[:, :, :]), flat(up_q[:, :, :])),
            (P, INNER, down_w[:, :], down_q[:, :])]
    for c in range(BLOCKS):
        jobs.append((P, 4 * E, flat(xn[:, 4 * c:4 * c + 4, :]), flat(x_q[:, 4 * c:4 * c + 4, :])))
    FIRST_HIDDEN = len(jobs)
    for i in range(PAIRS):
        jobs.append((P, widest, flat(hidden[:, i % 2, :, :]), flat(hidden_q[:, i % 2, :, :])))

    def source_ready(engine, n):
        if n < FIRST_HIDDEN:
            engine.wait_ge(loaded, 48)
        else:
            engine.wait_ge(hidden_ready, n - FIRST_HIDDEN + 1)

    def blocks(t, parts, slot, width):
        return t[0:parts, slot, 0:width].rearrange("p (b c) -> p b c", c=FP4_BLOCK)

    def spread(t, parts, slot, width):
        n = width // FP4_BLOCK
        return t[0:parts, slot, 0:n].unsqueeze(2).broadcast_to([parts, n, FP4_BLOCK])

    @block.sync
    def _(sp):
        sp.dma_start(gate_w[:, :, :], gate_in.rearrange("(c p) e -> p c e", p=CHUNK)).then_inc(loaded, 16)
        sp.dma_start(up_w[:, :, :], up_in.rearrange("(c p) e -> p c e", p=CHUNK)).then_inc(loaded, 16)
        sp.dma_start(down_w[:, :], down_in).then_inc(loaded, 16)

    @block.vector
    def _(dve):
        steps = 0

        def then(instruction):
            nonlocal steps
            steps += 1
            instruction.then_inc(chain, 1)
            dve.wait_ge(chain, steps)

        def levels(n):
            parts, width, source, _ = jobs[n]
            slot = n % 2
            nb = width // FP4_BLOCK
            source_ready(dve, n)
            if n >= 2:
                dve.wait_ge(quantised, n - 1)
            sc, inv = scale[0:parts, slot, 0:nb], inverse[0:parts, slot, 0:nb]
            then(dve.tensor_reduce(sc, source.rearrange("p (b c) -> p b c", c=FP4_BLOCK), AX.X, ALU.max,
                                   apply_absolute_value=True))
            then(dve.tensor_scalar(sc, sc, 1.0 / 6.0, 1e-12, ALU.mult, ALU.max))
            dve.tensor_scalar(half_scale[0:parts, slot, 0:nb], sc, 0.5, None, ALU.mult)
            then(dve.reciprocal(inv, sc))
            dve.wait_ge(sized, n + 1)
            over = size[0:parts, slot, 0:width]
            then(dve.tensor_tensor(blocks(size, parts, slot, width), blocks(size, parts, slot, width),
                                   spread(inverse, parts, slot, width), ALU.mult))
            out = level[0:parts, slot, 0:width]
            then(dve.tensor_scalar(out, over, FP4_MIDDLES[6], 2.0, ALU.is_gt, ALU.mult))
            then(dve.scalar_tensor_tensor(out, over, FP4_MIDDLES[5], out, ALU.is_gt, ALU.add))
            then(dve.scalar_tensor_tensor(out, over, FP4_MIDDLES[4], out, ALU.is_gt, ALU.add))
            then(dve.tensor_scalar(out, out, 2.0, None, ALU.mult))
            for middle in FP4_MIDDLES[3:0:-1]:
                then(dve.scalar_tensor_tensor(out, over, middle, out, ALU.is_gt, ALU.add))
            dve.scalar_tensor_tensor(out, over, FP4_MIDDLES[0], out, ALU.is_gt, ALU.add).then_inc(levelled, 1)

        for n in range(FIRST_HIDDEN):
            levels(n)
        for i in range(PAIRS + 1):
            if i < PAIRS:
                dve.wait_ge(silu_ready, i + 1)
                dve.wait_ge(up_ready, 2 * i + 2)
                if i >= 2:
                    dve.wait_ge(quantised, FIRST_HIDDEN + i - 1)
                dve.tensor_tensor(hidden[:, i % 2, :, :], silu[:, :, :], upped[:, :, 0:INNER],
                                  ALU.mult).then_inc(hidden_ready, 1)
                levels(FIRST_HIDDEN + i)
            if i >= 1:
                dve.wait_ge(down_ready, i)
                rows = x[:, 2 * (i - 1):2 * i, :]
                dve.tensor_tensor(rows, rows, downed[:, :, 0:E], ALU.add).then_inc(added, 1)

    @block.gpsimd
    def _(pool):
        for n, (parts, width, _, result) in enumerate(jobs):
            slot = n % 2
            pool.wait_ge(levelled, n + 1)
            pool.wait_ge(sized, n + 1)
            if n >= FIRST_HIDDEN + 2:
                pool.wait_ge(turned_full, TURNS_BEFORE + n - FIRST_HIDDEN - 1)
            out = level[0:parts, slot, 0:width]
            pool.tensor_tensor(out, out, sign[0:parts, slot, 0:width], ALU.mult).then_inc(signed, 1)
            pool.wait_ge(signed, n + 1)
            pool.tensor_tensor(result.rearrange("p (b c) -> p b c", c=FP4_BLOCK), blocks(level, parts, slot, width),
                               spread(half_scale, parts, slot, width), ALU.mult).then_inc(quantised, 1)

    @block.scalar
    def _(act):
        def magnitudes(n):
            parts, width, source, _ = jobs[n]
            slot = n % 2
            source_ready(act, n)
            if n >= 2:
                act.wait_ge(quantised, n - 1)
                act.wait_ge(levelled, n - 1)
            act.activation(size[0:parts, slot, 0:width], source, ACT.Abs)
            act.activation(sign[0:parts, slot, 0:width], source, ACT.Sign).then_inc(sized, 1)

        def swish(i):
            act.wait_ge(gate_ready, 2 * i + 2)
            if i >= 1:
                act.wait_ge(hidden_ready, i)
            act.activation(silu[:, :, :], gated[:, :, 0:INNER], ACT.Silu).then_inc(silu_ready, 1)

        for n in range(3):
            magnitudes(n)
        for n, (out, parts, width) in enumerate(((gate_t[:, :], P, INNER), (up_t[:, :], P, INNER),
                                                 (flat(down_t[:, :, :]), CHUNK, QB))):
            magnitudes(n + 3)
            act.wait_ge(turned_full, n + 1)
            act.activation(out, turned[0:parts, n % 2, 0:width], ACT.Copy).then_inc(turned_free, 1)
        magnitudes(6)
        for c in range(BLOCKS):
            act.wait_ge(turned_full, 3 + c + 1)
            act.activation(x_t[:, c * QB:(c + 1) * QB], turned[:, (3 + c) % 2, :], ACT.Copy).then_inc(turned_free, 1)
        swish(0)
        magnitudes(FIRST_HIDDEN)
        for i in range(PAIRS):
            if i + 1 < PAIRS:
                swish(i + 1)
                magnitudes(FIRST_HIDDEN + i + 1)
            act.wait_ge(turned_full, TURNS_BEFORE + i + 1)
            if i >= 2:
                act.wait_ge(down_ready, i - 1)
            act.activation(hidden_t[:, i % 2, :, :], turned[0:CHUNK, :, :], ACT.Copy).then_inc(turned_free, 1)

    @block.tensor
    def _(pe):
        def turn(n, sources, out, parts):
            if n >= 2:
                pe.wait_ge(turned_free, n - 1)
            for i, source in enumerate(sources):
                last = pe.transpose(out(i), source, identity[0:parts, 0:parts])
            last.then_inc(turned_full, 1)

        for n, source in enumerate((gate_q, up_q)):
            pe.wait_ge(quantised, n + 1)
            turn(n, [source[:, c, :] for c in range(CHUNKS)],
                 lambda c, n=n: turned[:, n, c * CHUNK:(c + 1) * CHUNK], CHUNK)
        pe.wait_ge(quantised, 3)
        turn(2, [down_q[:, c * CHUNK:(c + 1) * CHUNK] for c in range(CHUNKS)],
             lambda c: turned[0:CHUNK, 0, c * P:(c + 1) * P], P)
        for b in range(BLOCKS):
            pe.wait_ge(quantised, 3 + b + 1)
            turn(3 + b, [x_q[:, 4 * b + i, :] for i in range(4)],
                 lambda i, b=b: turned[:, (3 + b) % 2, i * P:(i + 1) * P], P)
        for i in range(PAIRS + 1):
            if i < PAIRS:
                for t in range(2):
                    if t == 0:
                        pe.wait_ge(turned_free, 3 + i // 2 + 1)
                        if i >= 1:
                            pe.wait_ge(silu_ready, i)
                    rows = x_t[:, (2 * i + t) * P:(2 * i + t + 1) * P]
                    pe.matmul(gated[:, t, 0:INNER], rows, gate_t[:, :], start=True, stop=True).then_inc(gate_ready, 1)
                for t in range(2):
                    if t == 0 and i >= 1:
                        pe.wait_ge(hidden_ready, i)
                    rows = x_t[:, (2 * i + t) * P:(2 * i + t + 1) * P]
                    pe.matmul(upped[:, t, 0:INNER], rows, up_t[:, :], start=True, stop=True).then_inc(up_ready, 1)
            if i >= 1:
                j = i - 1
                pe.wait_ge(quantised, FIRST_HIDDEN + j + 1)
                pe.wait_ge(turned_free, TURNS_BEFORE + j)
                for t in range(2):
                    for c in range(CHUNKS):
                        last = pe.transpose(turned[0:CHUNK, t, c * P:(c + 1) * P],
                                            hidden_q[:, j % 2, t, c * CHUNK:(c + 1) * CHUNK], identity[:, :])
                last.then_inc(turned_full, 1)
                pe.wait_ge(turned_free, TURNS_BEFORE + j + 1)
                if j >= 1:
                    pe.wait_ge(added, j)
                for t in range(2):
                    for c in range(CHUNKS):
                        last = pe.matmul(downed[:, t, 0:E], hidden_t[:, j % 2, t, c * P:(c + 1) * P],
                                         down_t[:, c, :], start=c == 0, stop=c == CHUNKS - 1)
                last.then_inc(down_ready, 1)


def causal_attention(nc, ctx, x, xnT, heads_in, heads_out, rotary_in, masks_in, table, fold, identity):
    def sb(name, shape, dt=F32):
        return ctx.enter_context(nc.sbuf_tensor(f"ca_{name}", shape, dt))

    def ps(name, shape):
        return ctx.enter_context(nc.psum_tensor(f"ca_{name}", shape, F32))

    def sem(name):
        return ctx.enter_context(nc.semaphore(f"ca_{name}"))

    RING = 8
    BANKS = 3
    SCALE = float(DH) ** -0.5
    head_w = sb("head_w", [P, 2, CW])
    head_o = sb("head_o", [P, 2, E])
    rotary = sb("rotary", [P, T])
    masks_f = sb("masks_f", [P, MASKS])
    masks = sb("masks", [P, MASKS], BF16)
    identity_b = sb("identity_b", [P, P], BF16)
    k_split = sb("k_split", [P, 2, T], F32R)
    k_high = sb("k_high", [P, 2, T], F32R)
    q_high = sb("q_high", [P, 4, QB], F32R)
    q_low = sb("q_low", [P, 4, QB], F32R)
    turned_k = sb("turned_k", [P, QB])
    turned_q = sb("turned_q", [P, QB])
    values = sb("values", [P, 2, TILES, DH])
    weights = sb("weights", [P, RING, 2, QB])
    sums = sb("sums", [P, 4, 2, QB])
    unscaled = sb("unscaled", [P, 2, QB])
    maxima = sb("maxima", [P, 2, 4, BLOCKS])
    top = sb("top", [P, 2, 4])
    neg_top = sb("neg_top", [P, 2, 4])
    aux_high = sb("aux_high", [P, 2, QB], F32R)
    rden = sb("rden", [P, 2, 4])
    ones = sb("ones", [P, 1])
    zeros = sb("zeros", [P, 1])
    primer = sb("primer", [P, 4])

    scores = ps("scores", [P, 2, 2 * QB])
    mixed = ps("mixed", [P, QB])
    side = ps("side", [P, BANKS, QB])

    loaded = sem("loaded")
    loaded_w = [sem("loaded_w0"), sem("loaded_w1")]
    loaded_o = [sem("loaded_o0"), sem("loaded_o1")]
    zeroed = sem("zeroed")
    primed = sem("primed")
    cast = sem("cast")
    score_full = [sem("score_full0"), sem("score_full1")]
    score_free = [sem("score_free0"), sem("score_free1")]
    side_full = [sem(f"side_full{i}") for i in range(BANKS)]
    side_free = [sem(f"side_free{i}") for i in range(BANKS)]
    rounded = sem("rounded")
    mixing = sem("mixing")
    summed = sem("summed")
    joined = sem("joined")
    copied = sem("copied")
    top_done = sem("top_done")
    neg_done = sem("neg_done")
    aux_rounded = sem("aux_rounded")
    rden_done = sem("rden_done")
    block = ctx.enter_context(nc.Block())

    TURNS = HEADS // 2
    rows = slice(DH, DH + AUXP)
    keep = table[rows, 68:69]

    def attended(j):
        return 2 * j + 2

    def maxed(j):
        return [(i, at, min(4, 4 * j + i + 1 - at)) for i in range(4) for at in range(0, 4 * j + i + 1, 4)]

    COST = {"S": 4, "A": 4, "K1": 4, "Q1": 4, "K2": 4, "Q2": 4, "Y": 4, "D": 4, "V": 8, "X": 3, "M": 1}

    def merge(one, other):
        total = [sum(COST[kind] for kind, i in stream) for stream in (one, other)]
        done, at, merged = [0, 0], [0, 0], []
        while at[0] < len(one) or at[1] < len(other):
            which = 0 if at[1] == len(other) or at[0] < len(one) and done[0] * total[1] <= done[1] * total[0] else 1
            item = (one, other)[which][at[which]]
            merged.append(item)
            done[which] += COST[item[0]]
            at[which] += 1
        return merged

    def order(b):
        n = attended(b % BLOCKS)
        main = []
        for u in range(n):
            main += [("A", u), ("S", u + 2)]
        found = [("X", m) for m in range(len(maxed((b + 2) % BLOCKS)))]
        others = [(kind, 0) for kind in ("K1", "Q1", "V", "K2", "Q2")]
        sides = merge(others, found) + [("D", 0), ("Y", 0), ("M", 0)]
        return merge(sides, main)

    PRE = 3 * 5 + len(maxed(0)) + len(maxed(1)) + 2
    side_at, unit_at = {}, {}
    for b in range(STEPS):
        for kind, i in order(b):
            if kind not in "SA":
                side_at[b, kind, i] = len(side_at)
        for u in range(attended(b % BLOCKS)):
            unit_at[b, u] = len(unit_at)
    SIDES, UNITS_TURN = len(side_at), len(unit_at)
    assert SIDES % BANKS == 0 and UNITS_TURN % RING == 0

    def unit_of(turn, b, u):
        n = unit_at[b, 0] + u
        return turn * UNITS_TURN + n, n

    def score_slot(turn, n):
        return n % 2, turn * (UNITS_TURN // 2) + n // 2

    def side_slot(turn, b, name, i=0):
        n = PRE + side_at[b, name, i]
        return n % BANKS, turn * (SIDES // BANKS) + n // BANKS

    def ahead():
        pieces = []
        for j in range(3):
            pieces += [(kind, j, 0) for kind in ("K1", "Q1", "K2", "Q2", "V")]
            if j < 2:
                pieces += [("X", j, m) for m in range(len(maxed(j)))] + [("M", j, 0)]
        assert len(pieces) == PRE
        return [(kind, j, i, (n % BANKS, n // BANKS)) for n, (kind, j, i) in enumerate(pieces)]

    def first_column(j, u):
        return 2 * P if 2 * u - 4 * j == 2 else 0

    @block.sync
    def _(sp):
        def load_w(parity, head):
            sp.dma_start(head_w[:, parity, :], heads_in[head]).then_inc(loaded_w[parity], 16)

        def load_o(parity, head):
            sp.dma_start(head_o[:, parity, :], heads_out[head]).then_inc(loaded_o[parity], 16)

        sp.dma_start(rotary[:, :], rotary_in).then_inc(loaded, 16)
        sp.dma_start(masks_f[:, :], masks_in).then_inc(loaded, 16)
        load_w(0, 0)
        load_w(1, 1)
        load_o(0, 0)
        load_o(1, 1)
        with sp.Fori(0, TURNS) as turn:
            last_uses = []
            for b, name in ((0, "Y"), (0, "V"), (4, "Y"), (4, "V")):
                bank, n = side_slot(turn, b, name)
                last_uses.append((side_free[bank], sp.snap(n + 1)))
            sp.wait_ge(*last_uses[0])
            load_o(1, turn * 2 + 1)
            sp.wait_ge(*last_uses[1])
            load_w(0, turn * 2 + 2)
            sp.wait_ge(*last_uses[2])
            load_o(0, turn * 2 + 2)
            sp.wait_ge(*last_uses[3])
            load_w(1, turn * 2 + 3)
        for s in loaded_w + loaded_o:
            sp.wait_ge(s, 16 * (TURNS + 1))

    @block.tensor
    def _(pe):
        def piece(slot):
            bank, n = slot
            if not (isinstance(n, int) and n == 0):
                pe.wait_ge(side_free[bank], n)
            return side[:, bank, :], side_full[bank]

        def rotate(slot, parity, col, j):
            out, full = piece(slot)
            pe.matmul(out, head_w[:, parity, col:col + P], xnT[:, j * QB:(j + 1) * QB],
                      start=True, stop=True).then_inc(full, 1)

        def fold_halves(slot, turned, last):
            out, full = piece(slot)
            pe.wait_ge(side_free[last[0]], last[1] + 1)
            pe.matmul(out, fold[:, :], turned[:, :], start=True, stop=True).then_inc(full, 1)

        def project_v(slot, parity, j):
            out, full = piece(slot)
            for i in range(4):
                t = 4 * j + i
                last = pe.matmul(out[:, i * DH:(i + 1) * DH], xnT[:, t * P:(t + 1) * P],
                                 head_w[:, parity, 2 * P:2 * P + DH], start=True, stop=True)
            last.then_inc(full, 1)

        def find_maxima(where, parity, slot, j, m):
            i, at, many = maxed(j)[m]
            out, full = piece(where)
            diagonal = at + many == 4 * j + i + 1
            last = pe.matmul(out[:, 0:many * P], q_high[:, slot, i * P:(i + 1) * P],
                             k_split[:, parity, at * P:(at + many) * P], start=True, stop=not diagonal)
            if diagonal:
                last = pe.matmul(out[:, (many - 1) * P:many * P], identity_b[:, :],
                                 masks[:, MASK_Q:MASK_Q + P], start=False, stop=True)
            last.then_inc(full, 1)

        def spread_maxima(slot, p, count):
            out, full = piece(slot)
            pe.wait_ge(neg_done, count)
            for i in range(4):
                last = pe.matmul(out[rows, i * P:(i + 1) * P], neg_top[:, p, i:i + 1].broadcast_to([P, AUXP]),
                                 identity[:, :], start=True, stop=True)
            last.then_inc(full, 1)

        def score(bank_count, parity, slot, j, u):
            bank, n = bank_count
            if not (isinstance(n, int) and n == 0):
                pe.wait_ge(score_free[bank], n)
            c0 = first_column(j, u)
            for half in range(2):
                c = 2 * u + half
                r = c - 4 * j
                at = half * QB
                pe.matmul(scores[:, bank, at + c0:at + QB], k_split[:, parity, c * P:(c + 1) * P],
                          q_high[:, slot, c0:QB], start=True, stop=False)
                last = pe.matmul(scores[:, bank, at + c0:at + QB], k_high[0:DH + AUXP, parity, c * P:(c + 1) * P],
                                 q_low[0:DH + AUXP, slot, c0:QB], start=False, stop=r < 0)
                if r >= 0:
                    end = (r + 1) * P
                    last = pe.matmul(scores[:, bank, at + c0:at + end], identity_b[:, :],
                                     masks[:, c0 + MASK_0 - r * P:end + MASK_0 - r * P], start=False, stop=True)
            last.then_inc(score_full[bank], 1)

        def mix(parity, ring, j, u):
            c0 = first_column(j, u)
            for half in range(2):
                last = pe.matmul(mixed[half * DH:(half + 1) * DH, c0:QB], values[:, parity, 2 * u + half, :],
                                 weights[:, ring, half, c0:QB], start=u == 0, stop=u == attended(j) - 1)
            last.then_inc(mixing, 1)

        def total(slot, q):
            out, full = piece(slot)
            for i in range(4):
                last = pe.matmul(out[:, i:i + 1], sums[:, q, 0, i * P:(i + 1) * P], ones[:, :],
                                 start=True, stop=True)
            last.then_inc(full, 1)

        def project_out(slot, p, parity, count):
            out, full = piece(slot)
            pe.wait_ge(copied, count)
            for i in range(4):
                last = pe.matmul(out[:, i * P:(i + 1) * P], unscaled[:, p, i * P:(i + 1) * P],
                                 head_o[:, parity, :], start=True, stop=True)
            last.then_inc(full, 1)

        pe.wait_ge(primed, 1)
        pe.wait_ge(cast, 2)
        pe.wait_ge(loaded_w[0], 16)
        pe.wait_ge(loaded_o[1], 16)
        firsts = {}
        for kind, j, i, slot in ahead():
            firsts[kind, j, i] = slot
            if kind == "K1":
                rotate(slot, 0, 0, j)
            elif kind == "Q1":
                rotate(slot, 0, P, j)
            elif kind == "K2":
                fold_halves(slot, turned_k, firsts["K1", j, 0])
            elif kind == "Q2":
                fold_halves(slot, turned_q, firsts["Q1", j, 0])
            elif kind == "V":
                project_v(slot, 0, j)
            elif kind == "X":
                if i == 0:
                    bank, n = firsts["Q2", j, 0]
                    pe.wait_ge(side_free[bank], n + 1)
                find_maxima(slot, 0, j, j, i)
            else:
                spread_maxima(slot, j, j + 1)
        bank, n = firsts["M", 0, 0]
        pe.wait_ge(side_free[bank], n + 1)
        for u in range(2):
            score((u, 0), 0, 0, 0, u)
        with pe.Fori(0, TURNS) as turn:
            for b in range(STEPS):
                parity, j = divmod(b, BLOCKS)
                step = turn * STEPS + b
                next_parity, next_j = (b + 1) // BLOCKS % 2, (b + 1) % BLOCKS
                found_parity, found_j = (b + 2) // BLOCKS % 2, (b + 2) % BLOCKS
                ahead_parity, ahead_j = (b + 3) // BLOCKS % 2, (b + 3) % BLOCKS
                for kind, i in order(b):
                    if kind not in "SA":
                        slot = side_slot(turn, b, kind, i)
                    if kind == "S":
                        number, n = unit_of(turn, b, i)
                        if i < attended(j):
                            score(score_slot(turn, n), parity, b % 4, j, i)
                        else:
                            score(score_slot(turn, n), next_parity, (b + 1) % 4, next_j, i - attended(j))
                    elif kind == "A":
                        if i == 0:
                            pe.wait_ge(copied, step + 2)
                        number, n = unit_of(turn, b, i)
                        bank, count = score_slot(turn, n)
                        pe.wait_ge(score_free[bank], count + 1)
                        mix(parity, n % RING, j, i)
                    elif kind == "X":
                        find_maxima(slot, found_parity, (b + 2) % 4, found_j, i)
                    elif kind == "K1":
                        if b == 1 or b == 5:
                            pe.wait_ge(loaded_w[ahead_parity], turn * 16 + (16 if b == 1 else 32))
                        rotate(slot, ahead_parity, 0, ahead_j)
                    elif kind == "Q1":
                        rotate(slot, ahead_parity, P, ahead_j)
                    elif kind == "K2":
                        fold_halves(slot, turned_k, side_slot(turn, b, "K1"))
                    elif kind == "Q2":
                        fold_halves(slot, turned_q, side_slot(turn, b, "Q1"))
                    elif kind == "V":
                        project_v(slot, ahead_parity, ahead_j)
                    elif kind == "M":
                        spread_maxima(slot, b % 2, step + 3)
                    elif kind == "D":
                        pe.wait_ge(joined, step + 1)
                        total(slot, (b - 1) % 4)
                    elif kind == "Y":
                        if b % BLOCKS == 1:
                            pe.wait_ge(loaded_o[parity], turn * 16 + 16 + 16 * parity)
                        project_out(slot, (b - 1) % 2, (b - 1) // BLOCKS % 2, step + 2)
        steps = TURNS * STEPS
        pe.wait_ge(joined, steps + 1)
        n = PRE + TURNS * SIDES
        total((n % BANKS, n // BANKS), 3)
        project_out(((n + 1) % BANKS, (n + 1) // BANKS), 1, 1, steps + 2)

    @block.scalar
    def _(act):
        def high_parts(slot, outs):
            bank, n = slot
            act.wait_ge(side_full[bank], n + 1)
            for out, parts in outs:
                last = act.activation(out, side[0:parts, bank, :], ACT.Copy)
            last.then_inc(rounded, 1)

        def key_outs(parity, j):
            cols = slice(j * QB, (j + 1) * QB)
            return [(k_high[0:DH, parity, cols], DH), (k_split[:, parity, cols], P)]

        def copy_mixed(p, units):
            act.wait_ge(mixing, units)
            act.activation(unscaled[:, p, :], mixed[:, :], ACT.Copy).then_inc(copied, 1)

        act.wait_ge(loaded, 32)
        act.activation(masks[:, :], masks_f[:, :], ACT.Copy).then_inc(cast, 1)
        act.activation(identity_b[:, :], identity[:, :], ACT.Copy).then_inc(cast, 1)
        act.wait_ge(primed, 1)
        def weigh(turn, j, i, n):
            bank, count = score_slot(turn, n)
            c0 = first_column(j, i)
            act.wait_ge(score_full[bank], count + 1)
            act.wait_ge(mixing, turn * UNITS_TURN + n + 1)
            act.wait_ge(summed, turn * UNITS_TURN + n + 1)
            act.activation(weights[:, n % RING, :, c0:QB],
                           scores[:, bank, :].rearrange("p (a q) -> p a q", a=2)[:, :, c0:QB],
                           ACT.Exp, scale=SCALE).then_inc(score_free[bank], 1)

        for kind, j, i, slot in ahead():
            if kind == "K2":
                high_parts(slot, key_outs(0, j))
            elif kind == "Q2":
                high_parts(slot, [(q_high[:, j, :], P)])
        for u in range(2):
            weigh(0, 0, u, u)
        with act.Fori(0, TURNS) as turn:
            for b in range(STEPS):
                j, next_j = b % BLOCKS, (b + 1) % BLOCKS
                ahead_parity, ahead_j = (b + 3) // BLOCKS % 2, (b + 3) % BLOCKS
                copy_mixed((b - 1) % 2, turn * UNITS_TURN + unit_at[b, 0] + RING)
                for kind, i in order(b):
                    if kind == "S":
                        number, n = unit_of(turn, b, i)
                        if i < attended(j):
                            weigh(turn, j, i, n)
                        else:
                            weigh(turn, next_j, i - attended(j), n)
                    elif kind == "K2":
                        high_parts(side_slot(turn, b, "K2"), key_outs(ahead_parity, ahead_j))
                    elif kind == "Q2":
                        high_parts(side_slot(turn, b, "Q2"), [(q_high[:, (b + 3) % 4, :], P)])
        copy_mixed(1, TURNS * UNITS_TURN + RING)

    @block.gpsimd
    def _(pool):
        pool.memset(ones[:, :], 1.0).then_inc(zeroed, 1)
        pool.wait_ge(zeroed, 1)
        pool.memset(zeros[:, :], 0.0).then_inc(zeroed, 1)
        pool.wait_ge(zeroed, 2)
        pool.memset(k_high[rows, :, :].bitcast(F32), 0.0).then_inc(zeroed, 1)
        pool.wait_ge(zeroed, 3)
        pool.memset(k_high[DH:DH + 2, :, :].bitcast(F32), 1.0).then_inc(primed, 1)

        def add_weights(bank_count, p, ring, j, u, units):
            bank, n = bank_count
            c0 = first_column(j, u)
            both = j > 0 and u == 1
            if u == 0 and j > 0:
                return
            pool.wait_ge(score_free[bank], n + 1)
            total, new = sums[:, p, :, c0:QB], weights[:, ring, :, c0:QB]
            if u == 0:
                pool.tensor_tensor(total, new, zeros[:, :].unsqueeze(1).broadcast_to([P, 2, QB]), ALU.add).then_inc(summed, 1)
            elif both:
                pool.tensor_tensor(total, weights[:, ring - 1, :, :], new, ALU.add).then_inc(summed, 2)
            else:
                pool.wait_ge(summed, units + RING)
                pool.tensor_tensor(total, total, new, ALU.add).then_inc(summed, 1)

        with pool.Fori(0, TURNS) as turn:
            for b in range(STEPS):
                j = b % BLOCKS
                for u in range(attended(j)):
                    number, n = unit_of(turn, b, u)
                    add_weights(score_slot(turn, n), b % 4, n % RING, j, u, number)
                pool.wait_ge(summed, turn * UNITS_TURN + unit_at[b, attended(j) - 1] + 1 + RING)
                pool.tensor_tensor(sums[:, b % 4, 0, :], sums[:, b % 4, 0, :], sums[:, b % 4, 1, :],
                                   ALU.add).then_inc(joined, 1)

    @block.vector
    def _(dve):
        def times_rotary(slot, turned, parity, bias, j):
            bank, n = slot
            dve.wait_ge(side_full[bank], n + 1)
            dve.scalar_tensor_tensor(turned[:, :], side[:, bank, :], head_w[:, parity, bias:bias + 1],
                                     rotary[:, j * QB:(j + 1) * QB], ALU.add, ALU.mult).then_inc(side_free[bank], 1)

        def low_parts(slot, part, out, high, count):
            bank, _ = slot
            dve.wait_ge(rounded, count)
            dve.tensor_tensor(out, side[part, bank, :], high.bitcast(F32), ALU.subtract).then_inc(side_free[bank], 1)

        def key_low(slot, parity, j, count):
            part = k_split[DH:P, parity, j * QB:(j + 1) * QB]
            low_parts(slot, slice(DH, P), part, part, count)

        def query_low(slot, p, count):
            low_parts(slot, slice(0, DH), q_low[0:DH, p, :], q_high[0:DH, p, :], count)

        def value(slot, parity, j):
            bank, n = slot
            dve.wait_ge(side_full[bank], n + 1)
            bias = head_w[:, parity, CV:CV + DH].unsqueeze(1).broadcast_to([P, 4, DH])
            dve.tensor_tensor(values[:, parity, 4 * j:4 * j + 4, :],
                              side[:, bank, 0:4 * DH].rearrange("p (t d) -> p t d", t=4), bias,
                              ALU.add).then_inc(side_free[bank], 1)

        def maximum(slot, p, j, m):
            bank, n = slot
            i, at, many = maxed(j)[m]
            dve.wait_ge(side_full[bank], n + 1)
            dve.tensor_reduce(maxima[:, p, i, at // 4:at // 4 + 1], side[:, bank, 0:many * P], AX.X,
                              ALU.max).then_inc(side_free[bank], 1)

        def negate_maxima(p, j, last, count):
            dve.wait_ge(side_free[last[0]], last[1] + 1)
            dve.tensor_reduce(top[:, p, :], maxima[:, p, :, 0:j + 1], AX.X, ALU.max).then_inc(top_done, 1)
            dve.wait_ge(top_done, count)
            dve.tensor_scalar(neg_top[:, p, :], top[:, p, :], -1.0, None, ALU.mult).then_inc(neg_done, 1)

        def split_maxima(slot, p, q, count):
            bank, n = slot
            dve.wait_ge(side_full[bank], n + 1)
            dve.tensor_copy(aux_high[rows, p, :], side[rows, bank, :]).then_inc(aux_rounded, 1)
            dve.wait_ge(aux_rounded, count)
            dve.scalar_tensor_tensor(q_low[rows, q, :], aux_high[rows, p, :].bitcast(F32), keep,
                                     side[rows, bank, :], ALU.mult, ALU.add).then_inc(side_free[bank], 1)

        def denominator(slot, p):
            bank, n = slot
            dve.wait_ge(side_full[bank], n + 1)
            dve.reciprocal(rden[:, p, :], side[:, bank, 0:4]).then_inc(side_free[bank], 1)

        def add_out(slot, p, j):
            bank, n = slot
            dve.wait_ge(side_full[bank], n + 1)
            for i in range(4):
                last = dve.scalar_tensor_tensor(x[:, 4 * j + i, :], side[:, bank, i * P:(i + 1) * P],
                                                rden[:, p, i:i + 1], x[:, 4 * j + i, :], ALU.mult, ALU.add)
            last.then_inc(side_free[bank], 1)

        dve.memset(mixed[:, :], 0.0).then_inc(mixing, RING)
        dve.memset(sums[:, 3, :, :], 1.0).then_inc(joined, 1)
        dve.memset(primer[:, 1:2], 0.0).then_inc(summed, RING)
        dve.memset(primer[:, 0:1], 0.0).then_inc(copied, 1)
        dve.wait_ge(loaded, 32)
        for kind, j, i, slot in ahead():
            if kind == "K1":
                times_rotary(slot, turned_k, 0, CB, j)
            elif kind == "Q1":
                times_rotary(slot, turned_q, 0, CB + 1, j)
            elif kind == "K2":
                key_low(slot, 0, j, 2 * j + 1)
            elif kind == "Q2":
                query_low(slot, j, 2 * j + 2)
            elif kind == "V":
                value(slot, 0, j)
            elif kind == "X":
                maximum(slot, j, j, i)
                if i == len(maxed(j)) - 1:
                    negate_maxima(j, j, slot, j + 1)
            else:
                split_maxima(slot, j, j, j + 1)
        with dve.Fori(0, TURNS) as turn:
            for b in range(STEPS):
                step = turn * STEPS + b
                found_j = (b + 2) % BLOCKS
                ahead_parity, ahead_j = (b + 3) // BLOCKS % 2, (b + 3) % BLOCKS
                for kind, i in order(b):
                    if kind in "SA":
                        continue
                    slot = side_slot(turn, b, kind, i)
                    if kind == "X":
                        maximum(slot, b % 2, found_j, i)
                        if i == len(maxed(found_j)) - 1:
                            negate_maxima(b % 2, found_j, slot, step + 3)
                    elif kind == "K1":
                        times_rotary(slot, turned_k, ahead_parity, CB, ahead_j)
                    elif kind == "Q1":
                        times_rotary(slot, turned_q, ahead_parity, CB + 1, ahead_j)
                    elif kind == "K2":
                        key_low(slot, ahead_parity, ahead_j, 2 * step + 7)
                    elif kind == "Q2":
                        query_low(slot, (b + 3) % 4, 2 * step + 8)
                    elif kind == "V":
                        value(slot, ahead_parity, ahead_j)
                    elif kind == "M":
                        split_maxima(slot, b % 2, (b + 2) % 4, step + 3)
                    elif kind == "D":
                        denominator(slot, (b - 1) % 2)
                    elif kind == "Y":
                        bank, n = side_slot(turn, b, "D")
                        dve.wait_ge(side_free[bank], n + 1)
                        add_out(slot, (b - 1) % 2, (b - 1) % BLOCKS)
        n = PRE + TURNS * SIDES
        denominator((n % BANKS, n // BANKS), 1)
        dve.wait_ge(side_free[n % BANKS], n // BANKS + 1)
        add_out(((n + 1) % BANKS, (n + 1) // BANKS), 1, BLOCKS - 1)


def fourier_feed_forward(nc, ctx, x, xnT, dft_in, freq_in, bias_row, out):
    def sb(name, shape, dt=F32):
        return ctx.enter_context(nc.sbuf_tensor(f"fo_{name}", shape, dt))

    def sem(name):
        return ctx.enter_context(nc.semaphore(f"fo_{name}"))

    dft = sb("dft", [P, 3, E])
    freq = sb("freq", [P, 2, E])
    parts = sb("parts", [P, 2, E])
    mixer = sb("mixer", [P, E])
    result = sb("result", [P, TILES, E])
    made = ctx.enter_context(nc.psum_tensor("fo_made", [P, QB], F32))
    product = ctx.enter_context(nc.psum_tensor("fo_product", [P, 2, QB], F32))
    loaded, first, split, second, mixer_done = (sem(n) for n in ("loaded", "first", "split", "second", "mixer_done"))
    multiplied, added, biased, stored = (sem(n) for n in ("multiplied", "added", "biased", "stored"))
    block = ctx.enter_context(nc.Block())

    @block.sync
    def _(sp):
        sp.dma_start(dft[:, :, :], dft_in).then_inc(loaded, 16)
        sp.dma_start(freq[:, :, :], freq_in).then_inc(loaded, 16)
        for b in range(BLOCKS):
            sp.wait_ge(added, b + 1)
            sp.dma_start(out[b * QB:(b + 1) * QB, :].rearrange("(t p) e -> p t e", p=P),
                         result[:, 4 * b:4 * b + 4, :]).then_inc(stored, 16)
        sp.wait_ge(stored, 16 * BLOCKS)

    @block.tensor
    def _(pe):
        pe.wait_ge(loaded, 32)
        pe.matmul(made[:, 0:E], freq[:, 0, :], dft[:, 0, :], start=True, stop=False)
        pe.matmul(made[:, 0:E], freq[:, 1, :], dft[:, 1, :], start=False, stop=True)
        pe.matmul(made[:, E:2 * E], freq[:, 1, :], dft[:, 0, :], start=True, stop=False)
        pe.matmul(made[:, E:2 * E], freq[:, 0, :], dft[:, 2, :], start=False, stop=True).then_inc(first, 1)
        pe.wait_ge(split, 1)
        pe.matmul(made[:, 2 * E:3 * E], parts[:, 0, :], dft[:, 0, :], start=True, stop=False)
        pe.matmul(made[:, 2 * E:3 * E], parts[:, 1, :], dft[:, 2, :], start=False, stop=True).then_inc(second, 1)
        pe.wait_ge(mixer_done, 1)
        for b in range(BLOCKS):
            if b >= 2:
                pe.wait_ge(added, b - 1)
            for i in range(4):
                t = 4 * b + i
                last = pe.matmul(product[:, b % 2, i * P:(i + 1) * P], xnT[:, t * P:(t + 1) * P],
                                 mixer[:, :], start=True, stop=True)
            last.then_inc(multiplied, 1)

    @block.scalar
    def _(act):
        act.wait_ge(first, 1)
        act.activation(parts[:, :, :], made[:, 0:2 * E], ACT.Copy).then_inc(split, 1)
        act.wait_ge(second, 1)
        act.activation(mixer[:, :], made[:, 2 * E:3 * E], ACT.Copy, scale=1.0 / E).then_inc(mixer_done, 1)

    @block.vector
    def _(dve):
        for b in range(BLOCKS):
            tiles = slice(4 * b, 4 * b + 4)
            row = bias_row.unsqueeze(1).broadcast_to([P, 4, E])
            dve.tensor_tensor(result[:, tiles, :], x[:, tiles, :], row, ALU.add).then_inc(biased, 1)
        for b in range(BLOCKS):
            tiles = slice(4 * b, 4 * b + 4)
            dve.wait_ge(multiplied, b + 1)
            dve.wait_ge(biased, b + 1)
            dve.tensor_tensor(result[:, tiles, :], result[:, tiles, :],
                              product[:, b % 2, :].rearrange("p (t e) -> p t e", t=4), ALU.add).then_inc(added, 1)



def run(nc, x_in, heads_in, heads_out, table_in, identity_in, rows_in, gate_in, up_in, down_in,
        causal_in, causal_out, rotary_in, masks_in, fold_in, dft_in, freq_in, out):
    with ExitStack() as ctx:
        x = ctx.enter_context(nc.sbuf_tensor("x", [P, TILES, E], F32))
        xnT = ctx.enter_context(nc.sbuf_tensor("xnT", [P, T], F32))
        table = ctx.enter_context(nc.sbuf_tensor("table", [P, TABLE], F32))
        fold = ctx.enter_context(nc.sbuf_tensor("fold", [P, P], F32))
        identity = ctx.enter_context(nc.sbuf_tensor("identity", [P, P], F32))
        bias_rows = ctx.enter_context(nc.sbuf_tensor("bias_rows", [P, 3, E], F32))
        loaded = ctx.enter_context(nc.semaphore("loaded"))
        stored = ctx.enter_context(nc.semaphore("stored"))
        biased = ctx.enter_context(nc.semaphore("biased"))
        with nc.Block() as block:
            @block.sync
            def _(sp):
                sp.dma_start(x[:, :, :], x_in.rearrange("(t p) e -> p t e", p=P)).then_inc(loaded, 16)
                sp.dma_start(identity[:, :], identity_in).then_inc(loaded, 16)
                sp.dma_start(table[:, :], table_in).then_inc(loaded, 16)
                sp.dma_start(bias_rows[:, :, :], rows_in).then_inc(loaded, 16)
                sp.dma_start(fold[:, :], fold_in).then_inc(loaded, 16)
                sp.wait_ge(loaded, 80)

        with ExitStack() as stage:
            layer_norm(nc, stage, x, xnT, identity, "ln0")

        def add_row(n):
            with nc.Block() as block:
                @block.vector
                def _(dve):
                    row = bias_rows[:, n, :].unsqueeze(1).broadcast_to([P, TILES, E])
                    dve.tensor_tensor(x[:, :, :], x[:, :, :], row, ALU.add)
        add_row(0)
        with ExitStack() as stage:
            distance_attention(nc, stage, x, xnT, heads_in, heads_out, table)
        with ExitStack() as stage:
            xn = layer_norm(nc, stage, x, None, identity, "ln1")
            fp4_feed_forward(nc, stage, x, xn, gate_in, up_in, down_in, identity)
        with ExitStack() as stage:
            layer_norm(nc, stage, x, xnT, identity, "ln2")
        add_row(1)
        with ExitStack() as stage:
            causal_attention(nc, stage, x, xnT, causal_in, causal_out, rotary_in, masks_in, table, fold, identity)
        with ExitStack() as stage:
            layer_norm(nc, stage, x, xnT, identity, "ln3")
        with ExitStack() as stage:
            fourier_feed_forward(nc, stage, x, xnT, dft_in, freq_in, bias_rows[:, 2, :], out)


def kernel(**inputs):
    from concourse import bacc
    from concourse.bass_utils import run_bass_kernel_spmd

    a = {k: np.asarray(v) for k, v in inputs.items()}
    w = a["L0_attn_W_in"].reshape(E, HEADS, 4, DH).transpose(1, 0, 2, 3)
    b = a["L0_attn_b_in"].reshape(HEADS, 4, DH)
    columns = np.stack([np.concatenate([b[:, i], b[:, i]], axis=1) for i in (0, 1, 3)], axis=2)
    v_rows = np.broadcast_to(b[:, 2][:, None, :], (HEADS, E, DH))
    packed = np.concatenate([w[:, :, 0], w[:, :, 0], w[:, :, 1], w[:, :, 1], w[:, :, 3], w[:, :, 3],
                             w[:, :, 2], columns, v_rows], axis=2)
    wo = a["L0_attn_W_out"].reshape(HEADS, DH, E)
    wo = np.concatenate([wo, wo], axis=1)
    table = np.zeros((P, TABLE), np.float32)
    table[0:DH, 2:4] = 1.0
    table[0:DH, AUXP:AUXP + 2] = 1.0
    table[DH:DH + AUX, 64] = [-0.5, -0.5, 0, 0]
    table[DH:DH + AUX, 65] = [1, 1, 0, -1]
    table[DH:DH + AUX, 66] = [0, 0, -0.5, -0.5]
    table[DH:DH + AUX, 67] = [0, -1, 1, 1]
    table[DH + 1, 68] = -1.0
    def head_rows(n):
        return a[f"L1_attn_{n}"].reshape(HEADS, DH, -1)

    swap = np.arange(DH) ^ 1
    wk, wq, wv = (head_rows(n).transpose(0, 2, 1) for n in ("wk", "wq", "wv"))
    bk, bq = (head_rows(n) for n in ("bk", "bq"))
    bv = np.broadcast_to(a["L1_attn_bv"].reshape(HEADS, 1, DH), (HEADS, E, DH))
    causal = np.concatenate([wk, wk[:, :, swap], wq, wq[:, :, swap], wv,
                             np.concatenate([bk, bk[:, swap]], axis=1), np.concatenate([bq, bq[:, swap]], axis=1),
                             bv], axis=2)
    co = a["L1_attn_wo"].T.reshape(HEADS, DH, E)
    co = np.concatenate([co, co], axis=1)
    theta = np.float32(10000.0) ** (np.arange(0, DH, 2, dtype=np.float32) / np.float32(DH))
    turns = np.arange(T, dtype=np.float32)[None, :] * (np.float32(1.0) / theta)[:, None]
    turns = np.concatenate([turns, turns]).astype(np.float32)
    sign = np.where(np.arange(DH) % 2 == 0, -1.0, 1.0)[:, None]
    rotary = np.concatenate([np.cos(turns), np.sin(turns) * sign]).astype(np.float32)
    masks = np.zeros((P, MASKS), np.float32)
    p = np.arange(P)[:, None]
    masks[:, :MASK_Q] = np.where(np.arange(MASK_Q)[None, :] - MASK_0 < p, -1e30, 0.0)
    masks[:, MASK_Q:] = np.where(np.arange(P)[None, :] > p, -1e30, 0.0)
    angle = 2.0 * np.pi * np.outer(np.arange(E), np.arange(E)) / E
    dft = np.stack([np.cos(angle), np.sin(angle), -np.sin(angle)], axis=1).astype(np.float32)
    rows = np.stack([np.broadcast_to(a[n], (P, E)) for n in ("L0_attn_b_out", "L1_attn_bo", "L1_ffn_bias")], axis=1)
    arrays = {
        "x": a["L0_attn_X"].reshape(T, E),
        "heads_in": np.concatenate([packed, packed[:2]]),
        "heads_out": np.concatenate([wo, wo[:2]]),
        "table": table,
        "identity": np.eye(P, dtype=np.float32),
        "rows": rows,
        "gate": a["L0_ffn_w_gate"],
        "up": a["L0_ffn_w_up"],
        "down": a["L0_ffn_w_down"],
        "causal": np.concatenate([causal, causal[:2]]),
        "causal_out": np.concatenate([co, co[:2]]),
        "rotary": rotary,
        "masks": masks,
        "fold": (np.arange(P)[:, None] % DH == np.arange(P)[None, :] % DH).astype(np.float32),
        "dft": dft,
        "freq": np.stack([a["L1_ffn_w_freq_real"], a["L1_ffn_w_freq_imag"]], axis=1),
    }
    arrays = {f"in_{k}": np.ascontiguousarray(v) for k, v in arrays.items()}
    nc = bacc.Bacc("TRN2", target_bir_lowering=False, num_devices=1)
    aps = [nc.dram_tensor(k, v.shape, mybir.dt.from_np(v.dtype), kind="ExternalInput").ap() for k, v in arrays.items()]
    out = nc.dram_tensor("out", (T, E), F32, kind="ExternalOutput").ap()
    run(nc, *aps, out)
    result = run_bass_kernel_spmd(nc, [arrays], core_ids=[0])
    return result.results[0]["out"].reshape(1, T, E)
```
